# Optimizing a Trainium2 kernel written in Bass

```python
import numpy as np
import jax
import jax.numpy as jnp

def _softmax(x, axis=-1):
    return jax.nn.softmax(x, axis=axis)

def _gelu(x):
    return jax.nn.gelu(x, approximate=True)

def _silu(x):
    return jax.nn.silu(x)

def _sigmoid(x):
    return jax.nn.sigmoid(x)

def _layernorm(x, axis=-1, eps=1e-05):
    m = jnp.mean(x, axis=axis, keepdims=True)
    v = jnp.var(x, axis=axis, keepdims=True)
    return (x - m) / jnp.sqrt(v + eps)

def _scatter_add(tgt, idx, src, axis=0):
    return tgt.at[idx].add(src)

def _segment_sum(src, seg, n):
    return jax.ops.segment_sum(src, seg, n)
kernel_name = 'mk_gnn_preln_d1_gnn_r8_a29f98'

def setup_inputs(seed: int=0):
    np.random.seed(seed)
    _w = jnp.asarray

    def _rec_inputs():
        import jax
        import jax.numpy as jnp
        _gk = jax.random.key(seed)
        x = -8.776e-05 + 1 * jax.random.normal(jax.random.fold_in(_gk, 1), (6250, 256), jnp.float32)
        _s = jax.random.randint(jax.random.fold_in(_gk, 2), (100000,), 0, 6250, jnp.int32)
        _d = jax.random.randint(jax.random.fold_in(_gk, 3), (100000,), 0, 6250, jnp.int32)
        _loop = jnp.arange(6250, dtype=jnp.int32)
        src = jnp.concatenate([_s, _d, _loop])
        dst = jnp.concatenate([_d, _s, _loop])
        _o = jnp.argsort(dst, stable=True)
        src = src[_o]
        dst = dst[_o]
        edge_attr_128 = -0.000128692 + 0.999872 * jax.random.normal(jax.random.fold_in(_gk, 11), (206250, 128), jnp.float32)
        return (x, src, dst, edge_attr_128)
    x, src, dst, edge_attr_128 = _rec_inputs()

    def _L0_gnn_setup():
        import jax, jax.numpy as jnp
        import numpy as np
        N_NODES = 2500
        N_EDGES = 40000
        NODE_DIM = 256
        EDGE_DIM = 128
        key = jax.random.key(seed)
        ks = jax.random.split(key, 10)
        s_n = 1.0 / np.sqrt(NODE_DIM)
        s_e = 1.0 / np.sqrt(EDGE_DIM)
        return {'node_features': jax.random.normal(ks[0], (N_NODES, NODE_DIM), jnp.float32), 'edge_features': jax.random.normal(ks[1], (N_EDGES, EDGE_DIM), jnp.float32), 'edge_indices': jax.random.randint(ks[2], (N_EDGES, 2), 0, N_NODES, jnp.int64), 'W_node': jax.random.uniform(ks[3], (NODE_DIM, NODE_DIM), jnp.float32, -s_n, s_n), 'b_node': jax.random.uniform(ks[4], (NODE_DIM,), jnp.float32, -s_n, s_n), 'W_edge': jax.random.uniform(ks[5], (EDGE_DIM, NODE_DIM), jnp.float32, -s_e, s_e), 'b_edge': jax.random.uniform(ks[6], (NODE_DIM,), jnp.float32, -s_e, s_e), 'W_out': jax.random.uniform(ks[7], (NODE_DIM, NODE_DIM), jnp.float32, -s_n, s_n), 'b_out': jax.random.uniform(ks[8], (NODE_DIM,), jnp.float32, -s_n, s_n)}
    _L0_gnn_all = _L0_gnn_setup()
    _L0_gnn_in = {k: v for k, v in _L0_gnn_all.items() if k in ('W_node', 'b_node', 'W_edge', 'b_edge', 'W_out', 'b_out')}
    del _L0_gnn_all
    return {'x': x, 'src': src, 'dst': dst, 'edge_attr_128': edge_attr_128, 'L0_gnn_W_node': _L0_gnn_in['W_node'], 'L0_gnn_b_node': _L0_gnn_in['b_node'], 'L0_gnn_W_edge': _L0_gnn_in['W_edge'], 'L0_gnn_b_edge': _L0_gnn_in['b_edge'], 'L0_gnn_W_out': _L0_gnn_in['W_out'], 'L0_gnn_b_out': _L0_gnn_in['b_out']}

def reference(x, src, dst, edge_attr_128, L0_gnn_W_node, L0_gnn_b_node, L0_gnn_W_edge, L0_gnn_b_edge, L0_gnn_W_out, L0_gnn_b_out):
    import jax
    import jax.numpy as jnp

    def _L0_gnn_ref(node_features, edge_features, edge_indices, W_node, b_node, W_edge, b_edge, W_out, b_out):
        import jax, jax.numpy as jnp
        import numpy as np
        N_NODES = 2500
        N_EDGES = 40000
        NODE_DIM = 256
        EDGE_DIM = 128
        node_t = node_features @ W_node + b_node
        edge_t = edge_features @ W_edge + b_edge
        src = edge_indices[:, 0]
        dst = edge_indices[:, 1]
        messages = node_t[src] * edge_t
        aggregated = jax.ops.segment_sum(messages, dst, num_segments=node_features.shape[0])
        return aggregated @ W_out + b_out
    edge_index_t = jnp.stack([src, dst], axis=1)
    h = jnp.maximum(_layernorm(x, axis=-1), 0.0)
    x = x + _L0_gnn_ref(h, edge_attr_128, edge_index_t, L0_gnn_W_node, L0_gnn_b_node, L0_gnn_W_edge, L0_gnn_b_edge, L0_gnn_W_out, L0_gnn_b_out)
    return x

_drawn_inputs = setup_inputs


def setup_inputs(seed=0):
    import zlib

    import numpy as np

    out = dict(_drawn_inputs(seed))
    spreads = {}
    factors = {}
    for name, (base, spread) in spreads.items():
        noise = np.random.default_rng([zlib.crc32(name.encode()), seed]).standard_normal(out[name].shape)
        drawn = base * np.exp(spread * noise) if base else spread * noise
        out[name] = jnp.asarray(drawn.astype(out[name].dtype))
    for name, factor in factors.items():
        out[name] = (out[name] * factor).astype(out[name].dtype)
    return out
```

```python
import numpy as np


def gnn_program(nc, x, src, dst, edge_attr, w_node, b_node, w_edge, b_edge, w_out, b_out, out):
    import concourse.bass as bass
    from concourse import mybir
    from contextlib import ExitStack

    F32, BF16, I32 = mybir.dt.float32, mybir.dt.bfloat16, mybir.dt.int32
    ALU = mybir.AluOpType
    ACT = mybir.ActivationFunctionType
    AX = mybir.AxisListType

    P = 128
    N, D = x.shape
    E, K = edge_attr.shape
    H = D // P
    EPS = 1e-5
    TPG = 8
    GE = TPG * P
    G = -(-E // GE)
    GF = E // GE
    GTAIL = E - GF * GE
    WIN = 64
    NT = -(-N // P)
    NTAIL = N - (NT - 1) * P
    NQ = -(-NT // 4)
    NPAIR = NT // 2
    BW = 512
    NB = -(-N // BW)
    AW = NB * BW
    assert G % 2 == 0 and NT % 8 == 1 and AW >= N + WIN and GTAIL > 0

    ctx = ExitStack()
    with ctx:
        def sb(name, shape, dt=F32):
            return ctx.enter_context(nc.sbuf_tensor(name, shape, dt))

        def ps(name, shape, dt=F32):
            return ctx.enter_context(nc.psum_tensor(name, shape, dt))

        def sem(name):
            return ctx.enter_context(nc.semaphore(name))

        node_table = nc.dram_tensor("node_table", (N, D), F32, kind="Internal").ap()

        x_sb = sb("x_sb", [P, NQ * 4 * D])
        aggT = sb("aggT", [P, H, AW])
        gathered = sb("gathered", [P, 2, TPG, D])
        h_sb = gathered[:, :, 0:4, :]
        e_sb = sb("e_sb", [P, 2, TPG * K])
        eT_sb = sb("eT_sb", [P, 2, 4, P])
        msg = sb("msg", [P, 4, 2, D])
        sel = sb("sel", [P, 2, TPG, WIN])
        src_all = sb("src_all", [P, G + 2, TPG], I32)
        src_stage = sb("src_stage", [P, 2, TPG], I32)
        dst_all = sb("dst_all", [P, G, TPG], I32)
        dst_f = sb("dst_f", [P, G, TPG])
        rel = sb("rel", [P, G, TPG])
        far = dst_all[:, :, :].bitcast(F32)
        base_f = sb("base_f", [P, G])
        base_i = sb("base_i", [1, G], I32)
        wn_sb = sb("wn_sb", [P, H, D])
        we_sb = sb("we_sb", [P, D])
        wo_sb = sb("wo_sb", [P, H, D])
        ident = sb("ident", [P, P])
        iota_w = sb("iota_w", [P, BW])
        ones = sb("ones", [P, P])
        ones3 = sb("ones3", [3, P], BF16)
        b_row = sb("b_row", [1, 3, D])
        b_part = sb("b_part", [1, 3, 3, D], BF16)
        b_rest = sb("b_rest", [1, 2, 3, D])
        bias3 = sb("bias3", [3, 3, D], BF16)
        eps_col = sb("eps_col", [P, 1])
        stat = sb("stat", [P, 2, 4, 6])
        mv = sb("mv", [P, 2, 4, 2])
        std = sb("std", [P, 2, 4])
        rstd = sb("rstd", [P, 2, 4])
        nmr = sb("nmr", [P, 2, 4])
        farmax = sb("farmax", [P, 1])
        farmax1 = sb("farmax1", [1, 1])
        far_flag = sb("far_flag", [1, 1], I32)
        s_idx = sb("s_idx", [P, 3], I32)
        s_f = sb("s_f", [P, 8])

        ps_T = [ps(f"ps_T{i}", [P, 4, P]) for i in range(2)]
        ps_E = [ps(f"ps_E{i}", [P, 2, D]) for i in range(2)]
        ps_A = [ps(f"ps_A{i}", [P, H, 256]) for i in range(2)]
        ps_B = [ps(f"ps_B{i}", [P, BW]) for i in range(2)]

        consts_set = sem("consts_set")
        ident_zero = sem("ident_zero")
        weights_loaded = sem("weights_loaded")
        bias_loaded = sem("bias_loaded")
        bias_split = sem("bias_split")
        bias3_loaded = sem("bias3_loaded")
        idx_set = sem("idx_set")
        src_loaded = sem("src_loaded")
        dst_loaded = sem("dst_loaded")
        prep = sem("prep")
        base_ready = sem("base_ready")
        farT_ready = sem("farT_ready")
        farmax_ready = sem("farmax_ready")
        flag_ready = sem("flag_ready")
        x_loaded = [sem(f"x_loaded{z}") for z in range(2)]
        stats_done = sem("stats_done")
        moments_done = sem("moments_done")
        std_done = sem("std_done")
        rstd_done = sem("rstd_done")
        scale_ready = sem("scale_ready")
        h_ready = sem("h_ready")
        h_turned = sem("h_turned")
        hT_ready = sem("hT_ready")
        node_mm = sem("node_mm")
        node_copied = sem("node_copied")
        node_stored = [sem(f"node_stored{z}") for z in range(2)]
        e_loaded = [sem(f"e_loaded{z}") for z in range(2)]
        idx_staged = sem("idx_staged")
        gather_turn = sem("gather_turn")
        vector_turn = sem("vector_turn")
        rows_landed = [[sem(f"rows_landed{s}{h}") for h in range(2)] for s in range(2)]
        e_turned = sem("e_turned")
        eT_ready = sem("eT_ready")
        edge_mm = sem("edge_mm")
        msg_ready = sem("msg_ready")
        sel_ready = sem("sel_ready")
        seg_done = sem("seg_done")
        flushed = sem("flushed")
        g_go = sem("g_go")
        g_loaded = sem("g_loaded")
        g_turn = sem("g_turn")
        g_rows = sem("g_rows")
        g_eT = sem("g_eT")
        g_eTc = sem("g_eTc")
        g_mm = sem("g_mm")
        g_chain = sem("g_chain")
        g_sel = sem("g_sel")
        g_sum = sem("g_sum")
        g_add = sem("g_add")
        agg_final = sem("agg_final")
        aT_ready = sem("aT_ready")
        out_mm = sem("out_mm")
        out_ready = sem("out_ready")
        out_stored = [sem(f"out_stored{z}") for z in range(2)]

        FIRST = 0
        node_pairs_total = NPAIR + 1

        def xt(t, n=1):
            return x_sb[:, bass.ds(t * D, n * D)]

        def rows_of(ap, first, tiles):
            return ap[bass.ds(first * P, tiles * P), :].rearrange("(t p) d -> p t d", p=P)

        block = ctx.enter_context(nc.Block())

        @block.sync
        def _(sp):
            sp.dma_start(b_row[0:1, 0, :], b_node.rearrange("(a d) -> a d", a=1)).then_inc(bias_loaded, 16)
            sp.dma_start(b_row[0:1, 1, :], b_edge.rearrange("(a d) -> a d", a=1)).then_inc(bias_loaded, 16)
            sp.dma_start(b_row[0:1, 2, :], b_out.rearrange("(a d) -> a d", a=1)).then_inc(bias_loaded, 16)
            sp.dma_start(wn_sb[:], w_node.rearrange("(h p) d -> p h d", p=P)).then_inc(weights_loaded, 16)
            sp.wait_ge(bias_split, 5)
            for k in range(3):
                sp.dma_start(bias3[k:k + 1, :, :], b_part[0:1, k, :, :]).then_inc(bias3_loaded, 16)
            sp.dma_start(we_sb[:], w_edge).then_inc(weights_loaded, 16)
            sp.dma_start(wo_sb[:], w_out.rearrange("(h p) d -> p h d", p=P)).then_inc(weights_loaded, 16)
            sp.wait_ge(idx_set, 2)
            tp, tr = GTAIL // TPG, GTAIL % TPG
            for arr, tile, landed in ((src, src_all, src_loaded), (dst, dst_all, dst_loaded)):
                sp.dma_start(tile[:, 0:GF, :], arr[0:GF * GE].rearrange("(g p j) -> p g j", p=P, j=TPG)
                             ).then_inc(landed, 16)
                sp.dma_start(tile[0:tp, GF, :], arr[GF * GE:GF * GE + tp * TPG].rearrange("(p j) -> p j", j=TPG)
                             ).then_inc(landed, 16)
                sp.dma_start(tile[tp:tp + 1, GF, 0:tr], arr[E - tr:E].rearrange("(p j) -> p j", p=1)
                             ).then_inc(landed, 16)
            for s in range(2):
                sp.dma_start(e_sb[:, s, :], edge_attr[s * GE:(s + 1) * GE, :].rearrange("(p j) k -> p (j k)", j=TPG)
                             ).then_inc(e_loaded[s], 16)

            def store_pair(i, u):
                v = 4 * i + u
                sp.wait_ge(node_copied, v + 1)
                sp.dma_start(rows_of(node_table, 2 * v, 2), msg[:, u % 2, :, :]).then_inc(node_stored[u % 2], 16)
            for u in range(4):
                store_pair(0, u)
            with sp.Fori(1, NPAIR // 4) as i:
                for u in range(4):
                    store_pair(i, u)
            sp.wait_ge(node_copied, NPAIR + 1)
            sp.dma_start(node_table[N - NTAIL:N, :], msg[0:NTAIL, 0, 0, :]).then_inc(node_stored[0], 16)

            def load_edges(i, s):
                g = 2 * i + s
                sp.wait_ge(e_turned, 2 * g - 2)
                sp.dma_start(e_sb[:, s, :], edge_attr[bass.ds(g * GE, GE), :].rearrange("(p j) k -> p (j k)", j=TPG)
                             ).then_inc(e_loaded[s], 16)
            with sp.Fori(1, G // 2 - 1) as i:
                load_edges(i, 0)
                load_edges(i, 1)
            load_edges(G // 2 - 1, 0)
            sp.wait_ge(e_turned, 2 * (G - 1) - 2)
            sp.dma_start(e_sb[0:tp, 1, :], edge_attr[GF * GE:GF * GE + tp * TPG, :].rearrange("(p j) k -> p (j k)", j=TPG)
                         ).then_inc(e_loaded[1], 16)
            sp.dma_start(e_sb[tp:tp + 1, 1, 0:tr * K], edge_attr[E - tr:E, :].rearrange("(p j) k -> p (j k)", p=1)
                         ).then_inc(e_loaded[1], 16)

            sp.wait_ge(flag_ready, 1)
            flag = sp.value_load(far_flag[0:1, 0:1], min_val=0, max_val=N)
            with sp.If(flag > 0):
                def load_tile(g, j, n):
                    tau = g * TPG + j
                    e0 = g * GE + j * P
                    sp.wait_ge(g_go, tau + 1)
                    sp.dma_start(e_sb[0:n, 0, 0:K], edge_attr[bass.ds(e0, n), :]).then_inc(g_loaded, 16)
                    sp.dma_start(s_idx[0:n, 0:1], src[bass.ds(e0, n)].rearrange("(p a) -> p a", a=1)).then_inc(g_loaded, 16)
                    sp.dma_start(s_idx[0:n, 1:2], dst[bass.ds(e0, n)].rearrange("(p a) -> p a", a=1)).then_inc(g_loaded, 16)
                    sp.dma_start(s_idx[:, 2:3], dst[bass.ds(g * GE, 1)].rearrange("(p a) -> p a", a=1)
                                 .to_broadcast([P, 1])).then_inc(g_loaded, 16)
                with sp.Fori(0, GF) as g:
                    with sp.Fori(0, TPG) as j:
                        load_tile(g, j, P)
                for j in range(-(-GTAIL // P)):
                    load_tile(GF, j, min(P, GTAIL - j * P))

            def store_out(i, u):
                v = 4 * i + u
                sp.wait_ge(out_ready, v + 1)
                sp.dma_start(rows_of(out, 2 * v, 2), msg[:, u % 2, :, :]).then_inc(out_stored[u % 2], 16)
            for u in range(4):
                store_out(0, u)
            with sp.Fori(1, NPAIR // 4) as i:
                for u in range(4):
                    store_out(i, u)
            sp.wait_ge(out_ready, NPAIR + 1)
            sp.dma_start(out[N - NTAIL:N, :], msg[0:NTAIL, 0, 0, :]).then_inc(out_stored[0], 16)
            sp.wait_ge(out_stored[0], 16 * (NPAIR // 2 + 1))
            sp.wait_ge(out_stored[1], 16 * (NPAIR // 2))

        @block.gpsimd
        def _(pool):
            def load_x(i, z):
                w = 2 * i + z
                pool.dma_start(xt(4 * w, 4).rearrange("p (t d) -> p t d", d=D), rows_of(x, 4 * w, 4)
                               ).then_inc(x_loaded[z], 16)
            load_x(0, 0)
            load_x(0, 1)
            pool.memset(ident[:], 0.0).then_inc(ident_zero, 1)
            pool.memset(ones[:], 1.0).then_inc(consts_set, 1)
            pool.memset(ones3[:], 1.0).then_inc(consts_set, 1)
            pool.memset(eps_col[:], EPS).then_inc(consts_set, 1)
            pool.wait_ge(ident_zero, 1)
            pool.affine_select(out=ident[:], in_=ident[:], compare_op=ALU.not_equal, fill=1.0, base=0,
                               pattern=[[-1, P]], channel_multiplier=1).then_inc(consts_set, 1)
            pool.memset(src_all[:], 0).then_inc(idx_set, 1)
            pool.memset(dst_all[:], -1).then_inc(idx_set, 1)
            pool.memset(x_sb[:, (NT - 1) * D:], 0.0).then_inc(consts_set, 1)
            pool.iota(iota_w[:], pattern=[[1, BW]], base=0, channel_multiplier=0,
                      allow_small_or_imprecise_dtypes=True).then_inc(consts_set, 1)

            with pool.Fori(1, NQ // 2) as i:
                for z in range(2):
                    pool.wait_ge(x_loaded[z], 16 * i)
                    pool.sem_inc(gather_turn, 1)
                    load_x(i, z)
            pool.wait_ge(consts_set, 6)
            pool.wait_ge(x_loaded[0], 16 * (NQ // 2))
            pool.dma_start(x_sb[0:NTAIL, (NT - 1) * D:NT * D], x[N - NTAIL:N, :]).then_inc(x_loaded[0], 16)
            pool.memset(aggT[:], 0.0).then_inc(consts_set, 1)

            pool.wait_ge(node_stored[0], 16 * (NPAIR // 2 + 1))
            pool.wait_ge(node_stored[1], 16 * (NPAIR // 2))

            def gather(i, s):
                pool.wait_ge(idx_staged, 2 * i + s + 1)
                pool.sem_inc(gather_turn, 1)
                for j in range(TPG):
                    pool.indirect_dma_start(out=gathered[:, s, j, :], out_offset=None, in_=node_table,
                                            in_offset=bass.IndirectOffsetOnAxis(ap=src_stage[:, s, j:j + 1], axis=0)
                                            ).then_inc(rows_landed[s][j // 4], 16)
            gather(0, 0)
            gather(0, 1)
            with pool.Fori(1, G // 2) as i:
                gather(i, 0)
                gather(i, 1)

            pool.wait_ge(flag_ready, 1)
            flag = pool.value_load(far_flag[0:1, 0:1], min_val=0, max_val=N)
            with pool.If(flag > 0):
                def gather_tile(tau):
                    pool.wait_ge(g_loaded, 64 * (tau + 1))
                    pool.sem_inc(g_turn, 1)
                    pool.indirect_dma_start(out=gathered[:, 0, 0, :], out_offset=None, in_=node_table,
                                            in_offset=bass.IndirectOffsetOnAxis(ap=s_idx[:, 0:1], axis=0)
                                            ).then_inc(g_rows, 16)
                with pool.Fori(0, -(-E // P)) as tau:
                    gather_tile(tau)

        @block.scalar
        def _(act):
            def deviation(i, z):
                act.wait_ge(moments_done, 2 * i + z + 1)
                nc.scalar.activation(std[:, z, :], mv[:, z, :, 1], ACT.Sqrt, bias=eps_col[:, 0:1]).then_inc(std_done, 1)

            def normalise(i, z):
                w = 2 * i + z
                act.wait_ge(scale_ready, w + 1)
                if not (isinstance(i, int) and i == FIRST):
                    act.wait_ge(h_turned, 2 * w - 2)
                for t in range(4):
                    last = nc.scalar.activation(h_sb[:, z, t, :], xt(4 * w + t), ACT.Relu,
                                                bias=nmr[:, z, t:t + 1], scale=rstd[:, z, t:t + 1])
                last.then_inc(h_ready, 1)

            def copy_hT(i, u):
                v = 4 * i + u
                act.wait_ge(h_turned, v + 1)
                if not (isinstance(i, int) and i == FIRST and u < 2):
                    act.wait_ge(node_mm, v - 1)
                nc.scalar.copy(eT_sb[:, u % 2, :, :], ps_T[u % 2][:]).then_inc(hT_ready, 1)

            def node_iteration(i):
                for z in range(2):
                    nz, ni = (1, i) if z == 0 else (0, i + 1)
                    copy_hT(i, 2 * z)
                    deviation(ni, nz)
                    copy_hT(i, 2 * z + 1)
                    normalise(ni, nz)
            act.wait_ge(consts_set, 6)
            deviation(0, 0)
            normalise(0, 0)
            node_iteration(0)
            with act.Fori(1, NPAIR // 4) as i:
                node_iteration(i)
            act.wait_ge(h_turned, NPAIR + 1)
            act.wait_ge(node_mm, NPAIR - 1)
            nc.scalar.copy(eT_sb[:, 0, 0:H, :], ps_T[0][:, 0:H, :]).then_inc(hT_ready, 1)

            def copy_eT(i, u):
                k = 4 * i + u
                act.wait_ge(e_turned, k + 1)
                if isinstance(i, int) and i == FIRST and u < 2:
                    act.wait_ge(node_mm, NPAIR + 1)
                else:
                    act.wait_ge(edge_mm, 2 * k - 2)
                nc.scalar.copy(eT_sb[:, u % 2, :, :], ps_T[u % 2][:]).then_inc(eT_ready, 1)
            for u in range(4):
                copy_eT(0, u)
            with act.Fori(1, G // 2) as i:
                for u in range(4):
                    copy_eT(i, u)

            act.wait_ge(flag_ready, 1)
            flag = act.value_load(far_flag[0:1, 0:1], min_val=0, max_val=N)
            with act.If(flag > 0):
                with act.Fori(0, -(-E // P)) as tau:
                    act.wait_ge(g_eT, tau + 1)
                    nc.scalar.copy(eT_sb[:, 0, 0, :], ps_T[0][:, 0, :]).then_inc(g_eTc, 1)

            act.wait_ge(agg_final, 1)

            def stage_agg(i, u):
                v = 4 * i + u
                if not (isinstance(i, int) and i == FIRST and u < 2):
                    act.wait_ge(out_mm, v - 1)
                nc.scalar.copy(eT_sb[:, u % 2, :, :].rearrange("p (h t) n -> p h (t n)", h=H),
                               aggT[:, :, bass.ds(2 * P * v, 2 * P)]).then_inc(aT_ready, 1)
            for u in range(4):
                stage_agg(0, u)
            with act.Fori(1, NPAIR // 4) as i:
                for u in range(4):
                    stage_agg(i, u)
            act.wait_ge(out_mm, NPAIR - 1)
            nc.scalar.copy(eT_sb[:, 0, :, :].rearrange("p (h t) n -> p h (t n)", h=H),
                           aggT[:, :, 2 * P * NPAIR:2 * P * (NPAIR + 1)]).then_inc(aT_ready, 1)

        @block.vector
        def _(dve):
            dve.wait_ge(bias_loaded, 48)
            nc.vector.tensor_copy(b_part[0:1, 0, :, :], b_row[:]).then_inc(bias_split, 1)
            dve.wait_ge(bias_split, 1)
            nc.vector.tensor_tensor(b_rest[0:1, 0, :, :], b_row[:], b_part[0:1, 0, :, :], ALU.subtract).then_inc(bias_split, 1)
            dve.wait_ge(bias_split, 2)
            nc.vector.tensor_copy(b_part[0:1, 1, :, :], b_rest[0:1, 0, :, :]).then_inc(bias_split, 1)
            dve.wait_ge(bias_split, 3)
            nc.vector.tensor_tensor(b_rest[0:1, 1, :, :], b_rest[0:1, 0, :, :], b_part[0:1, 1, :, :], ALU.subtract
                                    ).then_inc(bias_split, 1)
            dve.wait_ge(bias_split, 4)
            nc.vector.tensor_copy(b_part[0:1, 2, :, :], b_rest[0:1, 1, :, :]).then_inc(bias_split, 1)

            def statistics(i, z):
                w = 2 * i + z
                dve.wait_ge(x_loaded[z], 16 * (i + 1))
                if not (isinstance(i, int) and i == FIRST):
                    dve.wait_ge(std_done, w - 1)
                for t in range(4):
                    last = nc.vector.bn_stats(stat[:, z, t, :], xt(4 * w + t))
                last.then_inc(stats_done, 1)
                dve.wait_ge(stats_done, w + 1)
                dve.sem_inc(vector_turn, 1)
                for t in range(4):
                    last = nc.vector.bn_aggr(mv[:, z, t, :], stat[:, z, t, :])
                last.then_inc(moments_done, 1)
                dve.wait_ge(std_done, w + 1)
                if not (isinstance(i, int) and i == FIRST):
                    dve.wait_ge(h_ready, w - 1)
                nc.vector.reciprocal(rstd[:, z, :], std[:, z, :]).then_inc(rstd_done, 1)
                dve.wait_ge(rstd_done, w + 1)
                nc.vector.scalar_tensor_tensor(out=nmr[:, z, :], in0=mv[:, z, :, 0], scalar=-1.0, in1=rstd[:, z, :],
                                               op0=ALU.mult, op1=ALU.mult).then_inc(scale_ready, 1)

            def copy_nodes(i, u):
                v = 4 * i + u
                dve.wait_ge(node_mm, v + 1)
                if not (isinstance(i, int) and i == FIRST and u < 2):
                    dve.wait_ge(node_stored[u % 2], 16 * (2 * i + u // 2))
                nc.vector.tensor_copy(msg[:, u % 2, :, :], ps_E[u % 2][:]).then_inc(node_copied, 1)

            def node_iteration(i):
                for z in range(2):
                    nz, ni = (1, i) if z == 0 else (0, i + 1)
                    statistics(ni, nz)
                    copy_nodes(i, 2 * z)
                    copy_nodes(i, 2 * z + 1)
            dve.wait_ge(consts_set, 5)
            statistics(0, 0)
            node_iteration(0)
            with dve.Fori(1, NPAIR // 4) as i:
                node_iteration(i)
            dve.wait_ge(node_mm, NPAIR + 1)
            dve.wait_ge(node_stored[0], 16 * (NPAIR // 2))
            nc.vector.tensor_copy(msg[:, 0, 0, :], ps_E[0][:, 0, :]).then_inc(node_copied, 1)

            dve.wait_ge(src_loaded, 48)
            for s in range(2):
                nc.vector.tensor_copy(src_stage[:, s, :], src_all[:, s, :]).then_inc(idx_staged, 1)
            dve.wait_ge(dst_loaded, 48)
            nc.vector.tensor_copy(dst_f[:], dst_all[:]).then_inc(prep, 1)
            dve.wait_ge(base_ready, 1)
            nc.vector.tensor_copy(base_f[:], ps_B[0][:, 0:G]).then_inc(prep, 1)
            dve.wait_ge(prep, 2)
            nc.vector.tensor_tensor(rel[:], dst_f[:], base_f[:].unsqueeze(2).to_broadcast([P, G, TPG]), ALU.subtract
                                    ).then_inc(prep, 1)

            def one_hot(i, s):
                g = 2 * i + s
                if not (isinstance(i, int) and i == FIRST):
                    dve.wait_ge(seg_done, 4 * g - 4)
                nc.vector.tensor_tensor(sel[:, s, :, :],
                                        iota_w[:, 0:WIN].unsqueeze(1).to_broadcast([P, TPG, WIN]),
                                        rel[:, bass.ds(g, 1), :].rearrange("p a j -> p (a j)").unsqueeze(2)
                                        .to_broadcast([P, TPG, WIN]),
                                        ALU.is_equal).then_inc(sel_ready, 1)

            def multiply(i, s, q):
                m = 8 * i + 4 * s + q
                if q % 2 == 0:
                    dve.wait_ge(rows_landed[s][q // 2], 64 * (i + 1))
                dve.wait_ge(edge_mm, m + 1)
                if not (isinstance(i, int) and i == FIRST and s == 0):
                    dve.wait_ge(seg_done, m - 3)
                nc.vector.tensor_tensor(msg[:, q, :, :], ps_E[q % 2][:], gathered[:, s, 2 * q:2 * q + 2, :], ALU.mult
                                        ).then_inc(msg_ready, 1)

            def flush(g, slot):
                base = dve.value_load(base_i[0:1, bass.ds(g, 1)], min_val=0, max_val=N - 1)
                dve.wait_ge(seg_done, 4 * g + 4)
                dve.wait_ge(flushed, g + 1)
                nc.vector.tensor_tensor(aggT[:, :, bass.ds(base, WIN)], aggT[:, :, bass.ds(base, WIN)],
                                        ps_A[slot][:, :, 0:WIN], ALU.add).then_inc(flushed, 1)

            def stage_indices(i, s):
                nc.vector.tensor_copy(src_stage[:, s, :],
                                      src_all[:, bass.ds(2 * i + s + 2, 1), :].rearrange("p a j -> p (a j)")
                                      ).then_inc(idx_staged, 1)

            def edge_iteration(i):
                first = isinstance(i, int) and i == FIRST
                for s in range(2):
                    one_hot(i, s)
                    multiply(i, s, 0)
                    if not (first and s == 0):
                        flush(2 * i + s - 1, 1 - s)
                    multiply(i, s, 1)
                    multiply(i, s, 2)
                    multiply(i, s, 3)
                    dve.wait_ge(msg_ready, 8 * i + 4 * s + 4)
                    stage_indices(i, s)

            nc.vector.tensor_copy(base_i[0:1, :], dst_f[0:1, :, 0]).then_inc(prep, 1)
            dve.wait_ge(prep, 4)
            dve.wait_ge(consts_set, 7)
            nc.vector.sem_inc(flushed, 1)
            edge_iteration(0)
            dve.wait_ge(prep, 4)
            nc.vector.tensor_scalar(far, rel[:], 0.0, float(WIN - 1), ALU.max, ALU.min).then_inc(prep, 1)
            dve.wait_ge(prep, 5)
            nc.vector.tensor_tensor(far, far, rel[:], ALU.not_equal).then_inc(prep, 1)
            dve.wait_ge(prep, 6)
            nc.vector.scalar_tensor_tensor(out=far, in0=dst_f[:], scalar=1.0, in1=far, op0=ALU.add, op1=ALU.mult
                                           ).then_inc(prep, 1)
            dve.wait_ge(prep, 7)
            nc.vector.tensor_reduce(farmax[:], far.rearrange("p g j -> p (g j)"), AX.X, ALU.max).then_inc(farmax_ready, 1)
            with dve.Fori(1, G // 2) as i:
                edge_iteration(i)
            flush(G - 1, 1)
            dve.wait_ge(flushed, G + 1)
            dve.wait_ge(farT_ready, 1)
            nc.vector.tensor_reduce(farmax1[:], ps_B[1][0:1, 0:P], AX.X, ALU.max).then_inc(prep, 1)
            dve.wait_ge(prep, 8)
            nc.vector.tensor_copy(far_flag[:], farmax1[:]).then_inc(flag_ready, 1)


            dve.wait_ge(flag_ready, 1)
            flag = dve.value_load(far_flag[0:1, 0:1], min_val=0, max_val=N)
            with dve.If(flag > 0):
                CH = 9

                def far_tile(tau):
                    done = [0]

                    def link(ins):
                        done[0] += 1
                        ins.then_inc(g_chain, 1)
                        dve.wait_ge(g_chain, CH * tau + done[0])
                    dve.wait_ge(g_loaded, 64 * (tau + 1))
                    link(nc.vector.tensor_copy(s_f[:, 0:2], s_idx[:, 1:3]))
                    link(nc.vector.tensor_tensor(s_f[:, 2:3], s_f[:, 0:1], s_f[:, 1:2], ALU.subtract))
                    link(nc.vector.tensor_scalar(s_f[:, 3:4], s_f[:, 2:3], 0.0, float(WIN - 1), ALU.max, ALU.min))
                    link(nc.vector.tensor_tensor(s_f[:, 3:4], s_f[:, 3:4], s_f[:, 2:3], ALU.not_equal))
                    link(nc.vector.tensor_scalar(s_f[:, 4:5], s_f[:, 0:1], 1.0, s_f[:, 3:4], ALU.add, ALU.mult))
                    link(nc.vector.tensor_scalar(s_f[:, 5:6], s_f[:, 4:5], -1.0, None, ALU.add))
                    dve.wait_ge(g_mm, tau + 1)
                    dve.wait_ge(g_rows, 16 * (tau + 1))
                    link(nc.vector.tensor_tensor(msg[:, 0, 0, :], ps_E[0][:, 0, :], gathered[:, 0, 0, :], ALU.mult))
                    dve.sem_inc(vector_turn, 1)
                    with dve.Fori(0, NB) as b:
                        k = tau * NB + b
                        nc.vector.tensor_scalar(sel[:, 0, :, :].rearrange("p j w -> p (j w)"), iota_w[:],
                                                s_f[:, 5:6], None, ALU.is_equal).then_inc(g_sel, 1)
                        dve.wait_ge(g_sel, 2 * k + 1)
                        nc.vector.tensor_scalar(s_f[:, 5:6], s_f[:, 5:6], -float(BW), None, ALU.add).then_inc(g_sel, 1)
                        dve.wait_ge(g_sel, 2 * k + 2)
                        dve.wait_ge(g_sum, k + 1)
                        for h in range(H):
                            last = nc.vector.tensor_tensor(aggT[:, h, bass.ds(b * BW, BW)], aggT[:, h, bass.ds(b * BW, BW)],
                                                           ps_B[h][:], ALU.add)
                        last.then_inc(g_add, 1)
                        dve.wait_ge(g_add, k + 1)
                    link(nc.vector.memset(s_idx[:, 0:1], 0))
                    link(nc.vector.memset(s_idx[:, 1:2], -1))
                    nc.vector.sem_inc(g_go, 1)
                nc.vector.sem_inc(g_go, 1)
                with dve.Fori(0, -(-E // P)) as tau:
                    far_tile(tau)
            nc.vector.sem_inc(agg_final, 1)

            def add_residual(i, u):
                v = 4 * i + u
                dve.wait_ge(out_mm, v + 1)
                if not (isinstance(i, int) and i == FIRST and u < 2):
                    dve.wait_ge(out_stored[u % 2], 16 * (2 * i + u // 2))
                nc.vector.tensor_tensor(msg[:, u % 2, :, :].rearrange("p t d -> p (t d)"),
                                        ps_E[u % 2][:].rearrange("p t d -> p (t d)"), xt(2 * v, 2), ALU.add
                                        ).then_inc(out_ready, 1)
            for u in range(4):
                add_residual(0, u)
            with dve.Fori(1, NPAIR // 4) as i:
                for u in range(4):
                    add_residual(i, u)
            dve.wait_ge(out_mm, NPAIR + 1)
            dve.wait_ge(out_stored[0], 16 * (NPAIR // 2))
            nc.vector.tensor_tensor(msg[:, 0, 0, :], ps_E[0][:, 0, :], xt(NT - 1), ALU.add).then_inc(out_ready, 1)

        @block.tensor
        def _(pe):
            def bias(dst_ps, which, stop=False):
                nc.tensor.matmul(dst_ps, ones3[:], bias3[:, which, :], start=True, stop=stop)

            def turn_h(i, u):
                v = 4 * i + u
                if u % 2 == 0:
                    pe.wait_ge(h_ready, 2 * i + u // 2 + 1)
                if not (isinstance(i, int) and i == FIRST and u < 2):
                    pe.wait_ge(hT_ready, v - 1)
                for t in range(2):
                    for h in range(H):
                        last = nc.tensor.transpose(ps_T[u % 2][:, 2 * t + h, :],
                                                   h_sb[:, u // 2, 2 * (u % 2) + t, h * P:(h + 1) * P], ident[:])
                last.then_inc(h_turned, 1)

            def node_product(i, u, tiles=2):
                v = 4 * i + u
                pe.wait_ge(hT_ready, v + 1)
                if not (isinstance(i, int) and i == FIRST and u < 2):
                    pe.wait_ge(node_copied, v - 1)
                for t in range(tiles):
                    bias(ps_E[u % 2][:, t, :], 0)
                    for h in range(H):
                        last = nc.tensor.matmul(ps_E[u % 2][:, t, :], eT_sb[:, u % 2, 2 * t + h, :], wn_sb[:, h, :],
                                                start=False, stop=(h == H - 1))
                last.then_inc(node_mm, 1)

            def node_iteration(i):
                for z in range(2):
                    turn_h(i, 2 * z)
                    turn_h(i, 2 * z + 1)
                    node_product(i, 2 * z)
                    node_product(i, 2 * z + 1)
            pe.wait_ge(consts_set, 6)
            pe.wait_ge(bias3_loaded, 48)
            pe.wait_ge(weights_loaded, 48)
            node_iteration(0)
            with pe.Fori(1, NPAIR // 4) as i:
                node_iteration(i)
            pe.wait_ge(h_ready, NQ)
            pe.wait_ge(hT_ready, NPAIR - 1)
            for h in range(H):
                last = nc.tensor.transpose(ps_T[0][:, h, :], h_sb[:, 0, 0, h * P:(h + 1) * P], ident[:])
            last.then_inc(h_turned, 1)
            node_product(NPAIR // 4, 0, tiles=1)

            pe.wait_ge(prep, 1)
            nc.tensor.matmul(ps_B[0][:, 0:G], ones[0:1, :], dst_f[0:1, :, 0], start=True, stop=True).then_inc(base_ready, 1)

            def turn_edges(i, u):
                k = 4 * i + u
                s = u // 2
                if u % 2 == 0:
                    if isinstance(i, int) and i == G // 2 - 1 and s == 1:
                        pe.wait_ge(e_loaded[s], 16 * (i + 2))
                    else:
                        pe.wait_ge(e_loaded[s], 16 * (i + 1))
                if isinstance(i, int) and i == FIRST and u < 2:
                    pe.wait_ge(hT_ready, NPAIR + 1)
                else:
                    pe.wait_ge(eT_ready, k - 1)
                for t in range(4):
                    j = 4 * (u % 2) + t
                    last = nc.tensor.transpose(ps_T[u % 2][:, t, :], e_sb[:, s, j * K:(j + 1) * K], ident[:])
                last.then_inc(e_turned, 1)

            def edge_product(i, u, r):
                m = 8 * i + 2 * u + r
                if r == 0:
                    pe.wait_ge(eT_ready, 4 * i + u + 1)
                if isinstance(i, int) and i == FIRST and u == 0:
                    pe.wait_ge(node_copied, NPAIR + 1)
                else:
                    pe.wait_ge(msg_ready, m - 1)
                for t in range(2):
                    bias(ps_E[r][:, t, :], 1)
                    last = nc.tensor.matmul(ps_E[r][:, t, :], eT_sb[:, u % 2, 2 * r + t, :], we_sb[:],
                                            start=False, stop=True)
                last.then_inc(edge_mm, 1)

            def sum_pair(i, u, r):
                m = 8 * i + 2 * u + r
                s, q = u // 2, 2 * (u % 2) + r
                g = 2 * i + s
                if q == 0:
                    pe.wait_ge(sel_ready, g + 1)
                    if not (isinstance(i, int) and i == FIRST):
                        pe.wait_ge(flushed, g)
                pe.wait_ge(msg_ready, m + 1)
                for t in range(2):
                    for h in range(H):
                        last = nc.tensor.matmul(ps_A[s][:, h, 0:WIN], msg[:, q, t, h * P:(h + 1) * P],
                                                sel[:, s, 2 * q + t, :],
                                                start=(q == 0 and t == 0 and h == 0),
                                                stop=(q == 3 and t == 1), skip_group_check=True)
                last.then_inc(seg_done, 1)

            def edge_iteration(i):
                for u in range(4):
                    turn_edges(i, u)
                    pi, pu = (i, u - 1) if u else (i - 1, 3)
                    if not (isinstance(i, int) and i == FIRST and u == 0):
                        sum_pair(pi, pu, 0)
                        sum_pair(pi, pu, 1)
                    edge_product(i, u, 0)
                    edge_product(i, u, 1)
            edge_iteration(0)
            with pe.Fori(1, G // 2 - 1) as i:
                edge_iteration(i)
            edge_iteration(G // 2 - 1)
            sum_pair(G // 2 - 1, 3, 0)
            sum_pair(G // 2 - 1, 3, 1)
            pe.wait_ge(farmax_ready, 1)
            nc.tensor.transpose(ps_B[1][0:1, 0:P], farmax[:], ident[:]).then_inc(farT_ready, 1)

            pe.wait_ge(flag_ready, 1)
            flag = pe.value_load(far_flag[0:1, 0:1], min_val=0, max_val=N)
            with pe.If(flag > 0):
                with pe.Fori(0, -(-E // P)) as tau:
                    pe.wait_ge(g_loaded, 64 * (tau + 1))
                    nc.tensor.transpose(ps_T[0][:, 0, :], e_sb[:, 0, 0:K], ident[:]).then_inc(g_eT, 1)
                    pe.wait_ge(g_eTc, tau + 1)
                    bias(ps_E[0][:, 0, :], 1)
                    nc.tensor.matmul(ps_E[0][:, 0, :], eT_sb[:, 0, 0, :], we_sb[:], start=False, stop=True
                                     ).then_inc(g_mm, 1)
                    with pe.Fori(0, NB) as b:
                        pe.wait_ge(g_sel, 2 * (tau * NB + b) + 1)
                        for h in range(H):
                            last = nc.tensor.matmul(ps_B[h][:], msg[:, 0, 0, h * P:(h + 1) * P],
                                                    sel[:, 0, :, :].rearrange("p j w -> p (j w)"), start=True, stop=True)
                        last.then_inc(g_sum, 1)

            def out_product(i, u, tiles=2):
                v = 4 * i + u
                pe.wait_ge(aT_ready, v + 1)
                if not (isinstance(i, int) and i == FIRST and u < 2):
                    pe.wait_ge(out_ready, v - 1)
                for t in range(tiles):
                    bias(ps_E[u % 2][:, t, :], 2)
                    for h in range(H):
                        last = nc.tensor.matmul(ps_E[u % 2][:, t, :], eT_sb[:, u % 2, 2 * h + t, :], wo_sb[:, h, :],
                                                start=False, stop=(h == H - 1))
                last.then_inc(out_mm, 1)
            for u in range(4):
                out_product(0, u)
            with pe.Fori(1, NPAIR // 4) as i:
                for u in range(4):
                    out_product(i, u)
            out_product(NPAIR // 4, 0, tiles=1)


_INS = ["x", "src", "dst", "edge_attr_128", "L0_gnn_W_node", "L0_gnn_b_node", "L0_gnn_W_edge", "L0_gnn_b_edge",
        "L0_gnn_W_out", "L0_gnn_b_out"]


def kernel(x, src, dst, edge_attr_128, L0_gnn_W_node, L0_gnn_b_node, L0_gnn_W_edge, L0_gnn_b_edge, L0_gnn_W_out,
           L0_gnn_b_out):
    import concourse.bacc as bacc
    from concourse import mybir
    from concourse.bass_utils import run_bass_kernel_spmd as run

    nc = bacc.Bacc("TRN2", target_bir_lowering=False, num_devices=1)
    values = (x, src, dst, edge_attr_128, L0_gnn_W_node, L0_gnn_b_node, L0_gnn_W_edge, L0_gnn_b_edge, L0_gnn_W_out,
              L0_gnn_b_out)
    arrays = {f"in_{n}": np.ascontiguousarray(a) for n, a in zip(_INS, values)}
    args = [nc.dram_tensor(n, a.shape, mybir.dt.from_np(a.dtype), kind="ExternalInput").ap() for n, a in arrays.items()]
    out = nc.dram_tensor("out", tuple(x.shape), mybir.dt.float32, kind="ExternalOutput").ap()
    gnn_program(nc, *args, out)
    return run(nc, [arrays], core_ids=[0]).results[0]["out"]
```

```python
import numpy as np


def gnn_program(nc, x, src, dst, edge_attr, w_node, b_node, w_edge, b_edge, w_out, b_out, out):
    import concourse.bass as bass
    from concourse import mybir
    from contextlib import ExitStack

    F32, BF16, I32 = mybir.dt.float32, mybir.dt.bfloat16, mybir.dt.int32
    ALU = mybir.AluOpType
    ACT = mybir.ActivationFunctionType
    AX = mybir.AxisListType

    P = 128
    N, D = x.shape
    E, K = edge_attr.shape
    H = D // P
    EPS = 1e-5
    TPG = 8
    GE = TPG * P
    G = -(-E // GE)
    GF = E // GE
    GTAIL = E - GF * GE
    QE = 4 * P
    KQ = -(-E // QE)
    WIN = 32
    IE = 2 * GE
    NT = -(-N // P)
    NTAIL = N - (NT - 1) * P
    NQ = -(-NT // 4)
    NPAIR = NT // 2
    BW = 512
    NB = -(-N // BW)
    AW = NB * BW
    TT = 4
    IT = G // 2
    NBLK = IT // 4
    PER = 2 * P
    EARLY = NBLK - 2
    assert G % 2 == 0 and NT % 8 == 1 and AW >= N + WIN and 0 < GTAIL <= QE
    assert AW >= 2 * IE and D == 2 * P
    assert IT == 4 * NBLK + 1 and NBLK >= 3 and EARLY == NPAIR - 1

    ctx = ExitStack()
    with ctx:
        def sb(name, shape, dt=F32):
            return ctx.enter_context(nc.sbuf_tensor(name, shape, dt))

        def ps(name, shape, dt=F32):
            return ctx.enter_context(nc.psum_tensor(name, shape, dt))

        def sem(name):
            return ctx.enter_context(nc.semaphore(name))

        node_table = nc.dram_tensor("node_table", (N, D), F32, kind="Internal").ap()

        x_sb = sb("x_sb", [P, NQ * 4 * D])
        aggT = sb("aggT", [P, H, AW])
        gathered = sb("gathered", [P, 2, TPG, D])
        h_sb = gathered[:, :, 0:4, :]
        e_sb = sb("e_sb", [P, 2, TPG * K])
        eT_sb = sb("eT_sb", [P, 2, 4, P])
        msg = sb("msg", [P, 4, 2, D])
        sel = sb("sel", [P, 2, 4, WIN])
        far_sel = sb("far_sel", [P, BW])
        idx_rows = aggT[:, 0, 0:2 * IE].rearrange("p (a e) -> p a e", a=2).bitcast(I32)
        idx_nums = aggT[:, 1, 0:2 * IE].rearrange("p (a e) -> p a e", a=2)
        src_all = sb("src_all", [P, 16, IT], I32)
        src_stage = sb("src_stage", [P, 2, TPG], I32)
        dst_f = sb("dst_f", [P, 16, IT])
        rel = sb("rel", [P, 16, IT])
        far = sb("far", [P, 16, IT])
        base_f = sb("base_f", [P, 4, IT])
        base_i = sb("base_i", [1, IT, 4], I32)
        wn_sb = sb("wn_sb", [P, H, D])
        we_sb = sb("we_sb", [P, D])
        wo_sb = sb("wo_sb", [P, H, D])
        ident = sb("ident", [P, P])
        iota_w = sb("iota_w", [P, BW])
        ones = sb("ones", [P, P])
        bias2 = sb("bias2", [P, 3, 2, D])
        aT_sb = sb("aT_sb", [P, H, 2, P])
        out_sb = sb("out_sb", [P, 2, D])
        settle_at = sb("settle_at", [1, 16 * (NBLK + 1)], I32)
        early = sb("early", [1, 3, 4 * IT])
        early_max = sb("early_max", [1, 2])
        eps_col = sb("eps_col", [P, 1])
        stat = sb("stat", [P, 2, 4, 6])
        mv = sb("mv", [P, 2, 4, 2])
        std = sb("std", [P, 2, 4])
        rstd = sb("rstd", [P, 2, 4])
        nmr = sb("nmr", [P, 2, 4])
        farmax = sb("farmax", [P, 1])
        farmax1 = sb("farmax1", [1, 1])
        far_flag = sb("far_flag", [1, 1], I32)
        redo_flag = sb("redo_flag", [1, 1], I32)
        s_idx = sb("s_idx", [P, 3], I32)
        s_f = sb("s_f", [P, 8])

        ps_T = [ps(f"ps_T{i}", [P, 4, P]) for i in range(2)]
        ps_E = [ps(f"ps_E{i}", [P, 2, D]) for i in range(2)]
        ps_A = [ps(f"ps_A{i}", [P, H, 256]) for i in range(2)]
        ps_B = [ps(f"ps_B{i}", [P, BW]) for i in range(2)]

        consts_set = sem("consts_set")
        ident_zero = sem("ident_zero")
        wn_loaded = sem("wn_loaded")
        weights_loaded = sem("weights_loaded")
        bias_loaded = sem("bias_loaded")
        idx_set = sem("idx_set")
        src_ready = sem("src_ready")
        prep = sem("prep")
        base_ready = sem("base_ready")
        farT_ready = sem("farT_ready")
        farmax_ready = sem("farmax_ready")
        flag_ready = sem("flag_ready")
        x_loaded = [sem(f"x_loaded{z}") for z in range(2)]
        stats_done = sem("stats_done")
        moments_done = sem("moments_done")
        std_done = sem("std_done")
        rstd_done = sem("rstd_done")
        scale_ready = sem("scale_ready")
        h_ready = sem("h_ready")
        h_turned = sem("h_turned")
        hT_ready = sem("hT_ready")
        node_mm = sem("node_mm")
        node_copied = sem("node_copied")
        node_stored = [sem(f"node_stored{z}") for z in range(2)]
        e_loaded = [sem(f"e_loaded{z}") for z in range(2)]
        idx_staged = sem("idx_staged")
        gather_turn = sem("gather_turn")
        vector_turn = sem("vector_turn")
        rows_landed = [[sem(f"rows_landed{s}{h}") for h in range(2)] for s in range(2)]
        e_turned = sem("e_turned")
        eT_ready = sem("eT_ready")
        edge_mm = sem("edge_mm")
        idx_loaded = sem("idx_loaded")
        nums_ready = sem("nums_ready")
        idx_turned = sem("idx_turned")
        edge_added = sem("edge_added")
        msg_ready = sem("msg_ready")
        sel_ready = sem("sel_ready")
        seg_done = sem("seg_done")
        flushed = sem("flushed")
        g_go = sem("g_go")
        g_loaded = sem("g_loaded")
        g_turn = sem("g_turn")
        g_rows = sem("g_rows")
        g_eT = sem("g_eT")
        g_eTc = sem("g_eTc")
        g_mm = sem("g_mm")
        g_chain = sem("g_chain")
        g_sel = sem("g_sel")
        g_sum = sem("g_sum")
        g_add = sem("g_add")
        aT_ready = sem("aT_ready")
        out_mm = sem("out_mm")
        out_summed = sem("out_summed")
        out_ready = sem("out_ready")
        out_stored = sem("out_stored")
        redo_go = sem("redo_go")
        redo_aT = sem("redo_aT")
        redo_mm = sem("redo_mm")
        redo_summed = sem("redo_summed")
        redo_ready = sem("redo_ready")
        redo_stored = sem("redo_stored")
        last_go = sem("last_go")
        last_aT = sem("last_aT")
        last_mm = sem("last_mm")
        last_summed = sem("last_summed")
        last_ready = sem("last_ready")
        last_stored = sem("last_stored")

        FIRST = 0
        node_pairs_total = NPAIR + 1

        def xt(t, n=1):
            return x_sb[:, bass.ds(t * D, n * D)]

        def rows_of(ap, first, tiles):
            return ap[bass.ds(first * P, tiles * P), :].rearrange("(t p) d -> p t d", p=P)

        block = ctx.enter_context(nc.Block())

        @block.sync
        def _(sp):
            sp.wait_ge(idx_set, 2)
            for a, arr in enumerate((src, dst)):
                sp.dma_start(idx_rows[0:IT - 1, a, :], arr[0:(IT - 1) * IE].rearrange("(r e) -> r e", e=IE)
                             ).then_inc(idx_loaded, 16)
                sp.dma_start(idx_rows[IT - 1:IT, a, 0:E - (IT - 1) * IE],
                             arr[(IT - 1) * IE:E].rearrange("(r e) -> r e", r=1)).then_inc(idx_loaded, 16)
            sp.dma_start(wn_sb[:], w_node.rearrange("(h p) d -> p h d", p=P)).then_inc(wn_loaded, 16)
            for k, b in enumerate((b_node, b_edge, b_out)):
                for t in range(2):
                    sp.dma_start(bias2[:, k, t, :], b.rearrange("(a d) -> a d", a=1).to_broadcast([P, D])
                                 ).then_inc(bias_loaded, 16)
            sp.dma_start(we_sb[:], w_edge).then_inc(weights_loaded, 16)
            sp.dma_start(wo_sb[:], w_out.rearrange("(h p) d -> p h d", p=P)).then_inc(weights_loaded, 16)
            for s in range(2):
                sp.dma_start(e_sb[:, s, :].rearrange("p (c n) -> p c n", c=2),
                             edge_attr[s * GE:(s + 1) * GE, :].rearrange("(c p j) k -> p c (j k)", c=2, j=4)
                             ).then_inc(e_loaded[s], 16)

            def store_pair(i, u):
                v = 4 * i + u
                sp.wait_ge(node_copied, v + 1)
                sp.dma_start(rows_of(node_table, 2 * v, 2), msg[:, u % 2, :, :]).then_inc(node_stored[u % 2], 16)
            for u in range(4):
                store_pair(0, u)
            with sp.Fori(1, NPAIR // 4) as i:
                for u in range(4):
                    store_pair(i, u)
            sp.wait_ge(node_copied, NPAIR + 1)
            sp.dma_start(node_table[N - NTAIL:N, :], msg[0:NTAIL, 0, 0, :]).then_inc(node_stored[0], 16)

            def load_edges(i, s):
                g = 2 * i + s
                sp.wait_ge(e_turned, 2 * g - 2)
                sp.dma_start(e_sb[:, s, :].rearrange("p (c n) -> p c n", c=2),
                             edge_attr[bass.ds(g * GE, GE), :].rearrange("(c p j) k -> p c (j k)", c=2, j=4)
                             ).then_inc(e_loaded[s], 16)
            with sp.Fori(1, G // 2 - 1) as i:
                load_edges(i, 0)
                load_edges(i, 1)
            load_edges(G // 2 - 1, 0)
            tp, tr = GTAIL // TT, GTAIL % TT
            sp.wait_ge(e_turned, 2 * (G - 1) - 2)
            sp.dma_start(e_sb[0:tp, 1, 0:TT * K], edge_attr[GF * GE:GF * GE + tp * TT, :].rearrange("(p j) k -> p (j k)", j=TT)
                         ).then_inc(e_loaded[1], 16)
            sp.dma_start(e_sb[tp:tp + 1, 1, 0:tr * K], edge_attr[E - tr:E, :].rearrange("(p j) k -> p (j k)", p=1)
                         ).then_inc(e_loaded[1], 16)

            sp.wait_ge(flag_ready, 1)
            flag = sp.value_load(far_flag[0:1, 0:1], min_val=0, max_val=N)
            with sp.If(flag > 0):
                def load_tile(k, j, n):
                    tau = k * 4 + j
                    e0 = k * QE + j * P
                    sp.wait_ge(g_go, tau + 1)
                    sp.dma_start(e_sb[0:n, 0, 0:K], edge_attr[bass.ds(e0, n), :]).then_inc(g_loaded, 16)
                    sp.dma_start(s_idx[0:n, 0:1], src[bass.ds(e0, n)].rearrange("(p a) -> p a", a=1)).then_inc(g_loaded, 16)
                    sp.dma_start(s_idx[0:n, 1:2], dst[bass.ds(e0, n)].rearrange("(p a) -> p a", a=1)).then_inc(g_loaded, 16)
                    sp.dma_start(s_idx[:, 2:3], dst[bass.ds(k * QE, 1)].rearrange("(p a) -> p a", a=1)
                                 .to_broadcast([P, 1])).then_inc(g_loaded, 16)
                with sp.Fori(0, E // QE) as k:
                    with sp.Fori(0, 4) as j:
                        load_tile(k, j, P)
                for j in range(-(-(E % QE) // P)):
                    load_tile(E // QE, j, min(P, E % QE - j * P))

            sp.wait_ge(last_ready, 1)
            sp.dma_start(rows_of(out, 2 * EARLY, 2), out_sb[:]).then_inc(last_stored, 16)
            sp.wait_ge(last_ready, 2)
            sp.dma_start(out[N - NTAIL:N, :], msg[0:NTAIL, 0, 0, :]).then_inc(last_stored, 16)
            sp.wait_ge(last_stored, 32)

        @block.gpsimd
        def _(pool):
            def load_x(i, z):
                w = 2 * i + z
                pool.dma_start(xt(4 * w, 4).rearrange("p (t d) -> p t d", d=D), rows_of(x, 4 * w, 4)
                               ).then_inc(x_loaded[z], 16)
            pool.memset(idx_rows[:, 0, E - (IT - 1) * IE:IE], 0).then_inc(idx_set, 1)
            pool.memset(idx_rows[:, 1, E - (IT - 1) * IE:IE], -1).then_inc(idx_set, 1)
            load_x(0, 0)
            load_x(0, 1)
            pool.memset(ident[:], 0.0).then_inc(ident_zero, 1)
            pool.memset(ones[:], 1.0).then_inc(consts_set, 1)
            pool.memset(eps_col[:], EPS).then_inc(consts_set, 1)
            pool.wait_ge(ident_zero, 1)
            pool.affine_select(out=ident[:], in_=ident[:], compare_op=ALU.not_equal, fill=1.0, base=0,
                               pattern=[[-1, P]], channel_multiplier=1).then_inc(consts_set, 1)
            pool.memset(x_sb[:, (NT - 1) * D:], 0.0).then_inc(consts_set, 1)
            pool.iota(iota_w[:], pattern=[[1, BW]], base=0, channel_multiplier=0,
                      allow_small_or_imprecise_dtypes=True).then_inc(consts_set, 1)

            pool.iota(settle_at[:], pattern=[[PER, NBLK + 1], [0, 16]], base=-PER, channel_multiplier=0
                      ).then_inc(consts_set, 1)

            with pool.Fori(1, NQ // 2) as i:
                for z in range(2):
                    pool.wait_ge(x_loaded[z], 16 * i)
                    pool.sem_inc(gather_turn, 1)
                    load_x(i, z)
            pool.wait_ge(consts_set, 6)
            pool.wait_ge(x_loaded[0], 16 * (NQ // 2))
            pool.dma_start(x_sb[0:NTAIL, (NT - 1) * D:NT * D], x[N - NTAIL:N, :]).then_inc(x_loaded[0], 16)
            pool.wait_ge(idx_turned, 8)
            pool.memset(aggT[:], 0.0).then_inc(consts_set, 1)

            pool.wait_ge(node_stored[0], 16 * (NPAIR // 2 + 1))
            pool.wait_ge(node_stored[1], 16 * (NPAIR // 2))

            def gather(i, s, tiles=TPG):
                pool.wait_ge(idx_staged, 2 * i + s + 1)
                for j in range(tiles):
                    if j % 4 == 0:
                        if not (isinstance(i, int) and i == FIRST):
                            pool.wait_ge(msg_ready, 8 * i + 4 * s + 2 * (j // 4) - 6)
                        pool.sem_inc(gather_turn, 1)
                    pool.indirect_dma_start(out=gathered[:, s, j, :], out_offset=None, in_=node_table,
                                            in_offset=bass.IndirectOffsetOnAxis(ap=src_stage[:, s, j:j + 1], axis=0)
                                            ).then_inc(rows_landed[s][j // 4], 16)
            gather(0, 0)
            gather(0, 1)
            with pool.Fori(1, IT - 1) as i:
                gather(i, 0)
                gather(i, 1)
            gather(IT - 1, 0)
            gather(IT - 1, 1, TT)

            pool.wait_ge(flag_ready, 1)
            flag = pool.value_load(far_flag[0:1, 0:1], min_val=0, max_val=N)
            with pool.If(flag > 0):
                def gather_tile(tau):
                    pool.wait_ge(g_loaded, 64 * (tau + 1))
                    pool.sem_inc(g_turn, 1)
                    pool.indirect_dma_start(out=gathered[:, 0, 0, :], out_offset=None, in_=node_table,
                                            in_offset=bass.IndirectOffsetOnAxis(ap=s_idx[:, 0:1], axis=0)
                                            ).then_inc(g_rows, 16)
                with pool.Fori(0, -(-E // P)) as tau:
                    gather_tile(tau)

        @block.scalar
        def _(act):
            def deviation(i, z):
                act.wait_ge(moments_done, 2 * i + z + 1)
                nc.scalar.activation(std[:, z, :], mv[:, z, :, 1], ACT.Sqrt, bias=eps_col[:, 0:1]).then_inc(std_done, 1)

            def normalise(i, z):
                w = 2 * i + z
                act.wait_ge(scale_ready, w + 1)
                if not (isinstance(i, int) and i == FIRST):
                    act.wait_ge(h_turned, 2 * w - 2)
                for t in range(4):
                    last = nc.scalar.activation(h_sb[:, z, t, :], xt(4 * w + t), ACT.Relu,
                                                bias=nmr[:, z, t:t + 1], scale=rstd[:, z, t:t + 1])
                last.then_inc(h_ready, 1)

            def copy_hT(i, u):
                v = 4 * i + u
                act.wait_ge(h_turned, v + 1)
                if not (isinstance(i, int) and i == FIRST and u < 2):
                    act.wait_ge(node_mm, v - 1)
                nc.scalar.copy(eT_sb[:, u % 2, :, :], ps_T[u % 2][:]).then_inc(hT_ready, 1)

            def node_iteration(i):
                for z in range(2):
                    nz, ni = (1, i) if z == 0 else (0, i + 1)
                    copy_hT(i, 2 * z)
                    deviation(ni, nz)
                    copy_hT(i, 2 * z + 1)
                    normalise(ni, nz)
            act.wait_ge(idx_loaded, 64)
            nc.scalar.copy(idx_nums[0:IT, 0, :], idx_rows[0:IT, 0, :]).then_inc(nums_ready, 1)
            act.wait_ge(idx_turned, 4)
            for c, bank in enumerate((ps_T[0], ps_T[1], ps_A[0], ps_A[1])):
                nc.scalar.copy(src_all[:, 4 * c:4 * c + 4, :], bank[:].rearrange("p a b -> p (a b)")[:, 0:4 * IT]
                               .rearrange("p (t r) -> p t r", t=4)).then_inc(src_ready, 1)
            act.wait_ge(consts_set, 6)
            deviation(0, 0)
            normalise(0, 0)
            node_iteration(0)
            with act.Fori(1, NPAIR // 4) as i:
                node_iteration(i)
            act.wait_ge(h_turned, NPAIR + 1)
            act.wait_ge(node_mm, NPAIR - 1)
            nc.scalar.copy(eT_sb[:, 0, 0:H, :], ps_T[0][:, 0:H, :]).then_inc(hT_ready, 1)

            def copy_eT(i, u):
                k = 4 * i + u
                act.wait_ge(e_turned, k + 1)
                if isinstance(i, int) and i == FIRST and u < 2:
                    act.wait_ge(node_mm, NPAIR + 1)
                else:
                    act.wait_ge(edge_mm, 2 * k - 2)
                nc.scalar.copy(eT_sb[:, u % 2, :, :], ps_T[u % 2][:]).then_inc(eT_ready, 1)
            def copies(lo, hi):
                with act.Fori(lo, hi) as i:
                    for u in range(4):
                        copy_eT(i, u)
            for u in range(4):
                copy_eT(0, u)
            copies(1, 8)
            with act.Fori(2, NBLK) as b:
                copies(b * 4, b * 4 + 1)
                act.wait_ge(flushed, 16 * b + 3)
                act.wait_ge(out_mm, b - 1)
                nc.scalar.copy(aT_sb[:].rearrange("p h t n -> p h (t n)"),
                               aggT[:, :, bass.ds(b * PER - 2 * PER, PER)]).then_inc(aT_ready, 1)
                copies(b * 4 + 1, b * 4 + 4)
                act.wait_ge(out_ready, b)
                act.dma_start(rows_of(out, 2 * b - 4, 2), out_sb[:]).then_inc(out_stored, 16)
            for u in range(3):
                copy_eT(IT - 1, u)

            act.wait_ge(flag_ready, 1)
            flag = act.value_load(far_flag[0:1, 0:1], min_val=0, max_val=N)
            with act.If(flag > 0):
                with act.Fori(0, -(-E // P)) as tau:
                    act.wait_ge(g_eT, tau + 1)
                    nc.scalar.copy(eT_sb[:, 0, 0, :], ps_T[0][:, 0, :]).then_inc(g_eTc, 1)

            act.wait_ge(last_go, 1)
            redo = act.value_load(redo_flag[0:1, 0:1], min_val=0, max_val=N)
            with act.If(redo > 0):
                with act.Fori(0, EARLY) as v:
                    act.wait_ge(redo_go, v + 1)
                    nc.scalar.copy(aT_sb[:].rearrange("p h t n -> p h (t n)"),
                                   aggT[:, :, bass.ds(v * PER, PER)]).then_inc(redo_aT, 1)
                    act.wait_ge(redo_ready, v + 1)
                    act.dma_start(rows_of(out, 2 * v, 2), out_sb[:]).then_inc(redo_stored, 16)
            act.wait_ge(last_go, 2)
            nc.scalar.copy(aT_sb[:].rearrange("p h t n -> p h (t n)"),
                           aggT[:, :, EARLY * PER:(EARLY + 1) * PER]).then_inc(last_aT, 1)
            nc.scalar.copy(eT_sb[:, 0, 0:H, :], aggT[:, :, NPAIR * PER:NPAIR * PER + P]).then_inc(last_aT, 1)

        @block.vector
        def _(dve):
            dve.wait_ge(idx_loaded, 64)
            nc.vector.tensor_copy(idx_nums[0:IT, 1, :], idx_rows[0:IT, 1, :]).then_inc(nums_ready, 1)
            dve.wait_ge(idx_turned, 8)
            for c, bank in enumerate((ps_E[0], ps_E[1], ps_B[0], ps_B[1])):
                flat = bank[:] if c > 1 else bank[:].rearrange("p a b -> p (a b)")
                nc.vector.tensor_copy(dst_f[:, 4 * c:4 * c + 4, :], flat[:, 0:4 * IT].rearrange("p (t r) -> p t r", t=4)
                                      ).then_inc(prep, 1)
            def statistics(i, z):
                w = 2 * i + z
                dve.wait_ge(x_loaded[z], 16 * (i + 1))
                if not (isinstance(i, int) and i == FIRST):
                    dve.wait_ge(std_done, w - 1)
                for t in range(4):
                    last = nc.vector.bn_stats(stat[:, z, t, :], xt(4 * w + t))
                last.then_inc(stats_done, 1)
                dve.wait_ge(stats_done, w + 1)
                dve.sem_inc(vector_turn, 1)
                for t in range(4):
                    last = nc.vector.bn_aggr(mv[:, z, t, :], stat[:, z, t, :])
                last.then_inc(moments_done, 1)
                dve.wait_ge(std_done, w + 1)
                if not (isinstance(i, int) and i == FIRST):
                    dve.wait_ge(h_ready, w - 1)
                nc.vector.reciprocal(rstd[:, z, :], std[:, z, :]).then_inc(rstd_done, 1)
                dve.wait_ge(rstd_done, w + 1)
                nc.vector.scalar_tensor_tensor(out=nmr[:, z, :], in0=mv[:, z, :, 0], scalar=-1.0, in1=rstd[:, z, :],
                                               op0=ALU.mult, op1=ALU.mult).then_inc(scale_ready, 1)

            def copy_nodes(i, u):
                v = 4 * i + u
                dve.wait_ge(node_mm, v + 1)
                if not (isinstance(i, int) and i == FIRST and u < 2):
                    dve.wait_ge(node_stored[u % 2], 16 * (2 * i + u // 2))
                nc.vector.tensor_tensor(msg[:, u % 2, :, :], ps_E[u % 2][:], bias2[:, 0, :, :], ALU.add
                                        ).then_inc(node_copied, 1)

            def node_iteration(i):
                for z in range(2):
                    nz, ni = (1, i) if z == 0 else (0, i + 1)
                    statistics(ni, nz)
                    copy_nodes(i, 2 * z)
                    copy_nodes(i, 2 * z + 1)
            dve.wait_ge(consts_set, 6)
            statistics(0, 0)
            dve.wait_ge(bias_loaded, 16 * 6)
            node_iteration(0)
            with dve.Fori(1, NPAIR // 4) as i:
                node_iteration(i)
            dve.wait_ge(node_mm, NPAIR + 1)
            dve.wait_ge(node_stored[0], 16 * (NPAIR // 2))
            nc.vector.tensor_tensor(msg[:, 0, 0, :], ps_E[0][:, 0, :], bias2[:, 0, 0, :], ALU.add).then_inc(node_copied, 1)

            dve.wait_ge(src_ready, 4)
            for s in range(2):
                nc.vector.tensor_copy(src_stage[:, s, :], src_all[:, 8 * s:8 * s + 8, 0]).then_inc(idx_staged, 1)
            dve.wait_ge(base_ready, 1)
            nc.vector.tensor_copy(base_f[:], ps_B[0][:, 0:4 * IT].rearrange("p (c r) -> p c r", c=4)).then_inc(prep, 1)
            dve.wait_ge(prep, 5)
            for c in range(4):
                nc.vector.tensor_tensor(rel[:, 4 * c:4 * c + 4, :], dst_f[:, 4 * c:4 * c + 4, :],
                                        base_f[:, c, :].unsqueeze(1).to_broadcast([P, 4, IT]), ALU.subtract
                                        ).then_inc(prep, 1)
            nc.vector.tensor_copy(base_i[:], base_f[0:1, :, :].rearrange("a c r -> a r c")).then_inc(prep, 1)
            dve.wait_ge(prep, 10)

            def one_hot(i, u):
                k = 4 * i + u
                if not (isinstance(i, int) and i == FIRST and u < 2):
                    dve.wait_ge(seg_done, 2 * k - 2)
                nc.vector.tensor_tensor(sel[:, u % 2, :, :],
                                        iota_w[:, 0:WIN].unsqueeze(1).to_broadcast([P, 4, WIN]),
                                        rel[:, 4 * u:4 * u + 4, bass.ds(i, 1)].to_broadcast([P, 4, WIN]),
                                        ALU.is_equal).then_inc(sel_ready, 1)

            def add_bias(i, u, r):
                m = 8 * i + 2 * u + r
                dve.wait_ge(edge_mm, m + 1)
                if not (isinstance(i, int) and i == FIRST and u < 2):
                    dve.wait_ge(seg_done, m - 3)
                nc.vector.tensor_tensor(msg[:, 2 * (u % 2) + r, :, :], ps_E[r][:], bias2[:, 1, :, :], ALU.add
                                        ).then_inc(edge_added, 1)

            def multiply(i, u, r):
                m = 8 * i + 2 * u + r
                s, h, q = u // 2, u % 2, 2 * (u % 2) + r
                if r == 0:
                    dve.wait_ge(rows_landed[s][h], 64 * (i + 1))
                dve.wait_ge(edge_added, m + 1)
                nc.vector.tensor_tensor(msg[:, q, :, :], msg[:, q, :, :], gathered[:, s, 2 * q:2 * q + 2, :], ALU.mult
                                        ).then_inc(msg_ready, 1)

            def flush(i, u):
                k = 4 * i + u
                base = dve.value_load(base_i[0:1, bass.ds(i, 1), u], min_val=0, max_val=N - 1)
                dve.wait_ge(seg_done, 2 * k + 2)
                dve.wait_ge(flushed, k + 1)
                nc.vector.tensor_tensor(aggT[:, :, bass.ds(base, WIN)], aggT[:, :, bass.ds(base, WIN)],
                                        ps_A[u % 2][:, :, 0:WIN], ALU.add).then_inc(flushed, 1)

            def stage_indices(i, s):
                nc.vector.tensor_copy(src_stage[:, s, :],
                                      src_all[:, 8 * s:8 * s + 8, bass.ds(i + 1, 1)].rearrange("p j a -> p (j a)")
                                      ).then_inc(idx_staged, 1)

            def edge_iteration(i):
                last = isinstance(i, int) and i == IT - 1
                for u in range(3 if last else 4):
                    add_bias(i, u, 0)
                    one_hot(i, u)
                    multiply(i, u, 0)
                    if not (isinstance(i, int) and i == FIRST and u == 0):
                        flush(*((i, u - 1) if u else (i - 1, 3)))
                    add_bias(i, u, 1)
                    if u % 2 == 1 and not last:
                        stage_indices(i, u // 2)
                    multiply(i, u, 1)

            dve.wait_ge(consts_set, 7)
            nc.vector.sem_inc(flushed, 1)
            dve.wait_ge(node_stored[0], 16 * (NPAIR // 2 + 1))
            dve.wait_ge(node_stored[1], 16 * (NPAIR // 2))
            edge_iteration(0)
            nc.vector.tensor_scalar(far[:], rel[:], 0.0, float(WIN - 1), ALU.max, ALU.min).then_inc(prep, 1)
            dve.wait_ge(prep, 11)
            nc.vector.tensor_tensor(far[:], far[:], rel[:], ALU.not_equal).then_inc(prep, 1)
            dve.wait_ge(prep, 12)
            nc.vector.scalar_tensor_tensor(out=far[:], in0=dst_f[:], scalar=1.0, in1=far[:], op0=ALU.add, op1=ALU.mult
                                           ).then_inc(prep, 1)
            dve.wait_ge(prep, 13)
            nc.vector.tensor_reduce(farmax[:], far[:].rearrange("p g j -> p (g j)"), AX.X, ALU.max).then_inc(farmax_ready, 1)
            nc.vector.tensor_copy(early[0:1, 0, 0:KQ - 2], settle_at[0:1, 0:KQ - 2]).then_inc(prep, 1)
            nc.vector.tensor_copy(early[0:1, 1, :], base_i[0:1, :, :].rearrange("a r c -> a (r c)")).then_inc(prep, 1)
            dve.wait_ge(prep, 15)
            nc.vector.tensor_tensor(early[0:1, 2, 0:KQ - 2], early[0:1, 0, 0:KQ - 2], early[0:1, 1, 2:KQ], ALU.is_gt
                                    ).then_inc(prep, 1)
            dve.wait_ge(prep, 16)
            nc.vector.tensor_reduce(early_max[0:1, 0:1], early[0:1, 2, 0:KQ - 2], AX.X, ALU.max).then_inc(prep, 1)

            def edge_iterations(lo, hi):
                with dve.Fori(lo, hi) as i:
                    edge_iteration(i)

            def residual(summed, k, tile_sum, x_tiles, bias, result, ready):
                nc.vector.tensor_tensor(tile_sum, tile_sum, x_tiles, ALU.add).then_inc(summed, 1)
                dve.wait_ge(summed, k)
                nc.vector.tensor_tensor(result, tile_sum, bias, ALU.add).then_inc(ready, 1)

            def pair_residual(summed, k, v, ready):
                residual(summed, k, ps_B[0][:], xt(2 * v, 2), bias2[:, 2, :, :].rearrange("p t d -> p (t d)"),
                         out_sb[:].rearrange("p t d -> p (t d)"), ready)

            def block_of_iterations(b):
                edge_iterations(b * 4, b * 4 + 3)
                dve.wait_ge(out_mm, b)
                if not isinstance(b, int):
                    dve.wait_ge(out_stored, 16 * (b - 2))
                pair_residual(out_summed, b - 1, b - 2, out_ready)
                edge_iterations(b * 4 + 3, b * 4 + 4)
            nc.vector.sem_inc(out_ready, 1)
            edge_iterations(1, 8)
            block_of_iterations(2)
            with dve.Fori(3, NBLK) as b:
                block_of_iterations(b)
            edge_iteration(IT - 1)
            flush(IT - 1, 2)
            dve.wait_ge(flushed, KQ + 1)
            dve.wait_ge(farT_ready, 1)
            nc.vector.tensor_reduce(farmax1[:], ps_B[1][0:1, 0:P], AX.X, ALU.max).then_inc(prep, 1)
            dve.wait_ge(prep, 18)
            nc.vector.tensor_tensor(early_max[0:1, 1:2], early_max[0:1, 0:1], farmax1[:], ALU.max).then_inc(prep, 1)
            dve.wait_ge(prep, 19)
            nc.vector.tensor_copy(redo_flag[:], early_max[0:1, 1:2]).then_inc(prep, 1)
            dve.wait_ge(prep, 20)
            nc.vector.tensor_copy(far_flag[:], farmax1[:]).then_inc(flag_ready, 1)


            dve.wait_ge(flag_ready, 1)
            flag = dve.value_load(far_flag[0:1, 0:1], min_val=0, max_val=N)
            with dve.If(flag > 0):
                CH = 10

                def far_tile(tau):
                    done = [0]

                    def link(ins):
                        done[0] += 1
                        ins.then_inc(g_chain, 1)
                        dve.wait_ge(g_chain, CH * tau + done[0])
                    dve.wait_ge(g_loaded, 64 * (tau + 1))
                    link(nc.vector.tensor_copy(s_f[:, 0:2], s_idx[:, 1:3]))
                    link(nc.vector.tensor_tensor(s_f[:, 2:3], s_f[:, 0:1], s_f[:, 1:2], ALU.subtract))
                    link(nc.vector.tensor_scalar(s_f[:, 3:4], s_f[:, 2:3], 0.0, float(WIN - 1), ALU.max, ALU.min))
                    link(nc.vector.tensor_tensor(s_f[:, 3:4], s_f[:, 3:4], s_f[:, 2:3], ALU.not_equal))
                    link(nc.vector.tensor_scalar(s_f[:, 4:5], s_f[:, 0:1], 1.0, s_f[:, 3:4], ALU.add, ALU.mult))
                    link(nc.vector.tensor_scalar(s_f[:, 5:6], s_f[:, 4:5], -1.0, None, ALU.add))
                    dve.wait_ge(g_mm, tau + 1)
                    dve.wait_ge(g_rows, 16 * (tau + 1))
                    link(nc.vector.tensor_tensor(msg[:, 0, 0, :], ps_E[0][:, 0, :], bias2[:, 1, 0, :], ALU.add))
                    link(nc.vector.tensor_tensor(msg[:, 0, 0, :], msg[:, 0, 0, :], gathered[:, 0, 0, :], ALU.mult))
                    dve.sem_inc(vector_turn, 1)
                    with dve.Fori(0, NB) as b:
                        k = tau * NB + b
                        nc.vector.tensor_scalar(far_sel[:], iota_w[:],
                                                s_f[:, 5:6], None, ALU.is_equal).then_inc(g_sel, 1)
                        dve.wait_ge(g_sel, 2 * k + 1)
                        nc.vector.tensor_scalar(s_f[:, 5:6], s_f[:, 5:6], -float(BW), None, ALU.add).then_inc(g_sel, 1)
                        dve.wait_ge(g_sel, 2 * k + 2)
                        dve.wait_ge(g_sum, k + 1)
                        for h in range(H):
                            last = nc.vector.tensor_tensor(aggT[:, h, bass.ds(b * BW, BW)], aggT[:, h, bass.ds(b * BW, BW)],
                                                           ps_B[h][:], ALU.add)
                        last.then_inc(g_add, 1)
                        dve.wait_ge(g_add, k + 1)
                    link(nc.vector.memset(s_idx[:, 0:1], 0))
                    link(nc.vector.memset(s_idx[:, 1:2], -1))
                    nc.vector.sem_inc(g_go, 1)
                nc.vector.sem_inc(g_go, 1)
                with dve.Fori(0, -(-E // P)) as tau:
                    far_tile(tau)
            dve.wait_ge(out_stored, 16 * EARLY)
            nc.vector.sem_inc(last_go, 1)

            redo = dve.value_load(redo_flag[0:1, 0:1], min_val=0, max_val=N)
            with dve.If(redo > 0):
                nc.vector.sem_inc(redo_go, 1)
                with dve.Fori(0, EARLY) as v:
                    dve.wait_ge(redo_mm, v + 1)
                    pair_residual(redo_summed, v + 1, v, redo_ready)
                    dve.wait_ge(redo_stored, 16 * (v + 1))
                    nc.vector.sem_inc(redo_go, 1)
            nc.vector.sem_inc(last_go, 1)
            dve.wait_ge(last_mm, 1)
            pair_residual(last_summed, 1, EARLY, last_ready)
            dve.wait_ge(last_mm, 2)
            residual(last_summed, 2, ps_E[0][:, 0, :], xt(NT - 1), bias2[:, 2, 0, :], msg[:, 0, 0, :], last_ready)

        @block.tensor
        def _(pe):
            def turn_h(i, u):
                v = 4 * i + u
                if u % 2 == 0:
                    pe.wait_ge(h_ready, 2 * i + u // 2 + 1)
                if not (isinstance(i, int) and i == FIRST and u < 2):
                    pe.wait_ge(hT_ready, v - 1)
                for t in range(2):
                    for h in range(H):
                        last = nc.tensor.transpose(ps_T[u % 2][:, 2 * t + h, :],
                                                   h_sb[:, u // 2, 2 * (u % 2) + t, h * P:(h + 1) * P], ident[:])
                last.then_inc(h_turned, 1)

            def node_product(i, u, tiles=2):
                v = 4 * i + u
                pe.wait_ge(hT_ready, v + 1)
                if not (isinstance(i, int) and i == FIRST and u < 2):
                    pe.wait_ge(node_copied, v - 1)
                for t in range(tiles):
                    for h in range(H):
                        last = nc.tensor.matmul(ps_E[u % 2][:, t, :], eT_sb[:, u % 2, 2 * t + h, :], wn_sb[:, h, :],
                                                start=(h == 0), stop=(h == H - 1))
                last.then_inc(node_mm, 1)

            def node_iteration(i):
                for z in range(2):
                    turn_h(i, 2 * z)
                    turn_h(i, 2 * z + 1)
                    node_product(i, 2 * z)
                    node_product(i, 2 * z + 1)
            pe.wait_ge(consts_set, 6)
            pe.wait_ge(nums_ready, 2)
            for a, banks in enumerate(((ps_T[0], ps_T[1], ps_A[0], ps_A[1]), (ps_E[0], ps_E[1], ps_B[0], ps_B[1]))):
                for c, bank in enumerate(banks):
                    flat = bank[:] if a == 1 and c > 1 else bank[:].rearrange("p a b -> p (a b)")
                    by_tile = idx_nums[0:IT, a, c * QE:(c + 1) * QE].rearrange("r (p t) -> r t p", t=4)
                    for t in range(4):
                        last = nc.tensor.transpose(flat[:, t * IT:(t + 1) * IT], by_tile[:, t, :], ident[0:IT, 0:IT])
                    last.then_inc(idx_turned, 1)
            pe.wait_ge(wn_loaded, 16)
            pe.wait_ge(src_ready, 4)
            pe.wait_ge(prep, 4)
            node_iteration(0)
            with pe.Fori(1, NPAIR // 4) as i:
                node_iteration(i)
            pe.wait_ge(h_ready, NQ)
            pe.wait_ge(hT_ready, NPAIR - 1)
            for h in range(H):
                last = nc.tensor.transpose(ps_T[0][:, h, :], h_sb[:, 0, 0, h * P:(h + 1) * P], ident[:])
            last.then_inc(h_turned, 1)
            node_product(NPAIR // 4, 0, tiles=1)

            nc.tensor.matmul(ps_B[0][:, 0:4 * IT], ones[0:1, :], dst_f[0:1, 0:16:4, :], start=True, stop=True
                             ).then_inc(base_ready, 1)

            def turn_edges(i, u):
                k = 4 * i + u
                s = u // 2
                if u % 2 == 0:
                    if isinstance(i, int) and i == IT - 1 and s == 1:
                        pe.wait_ge(e_loaded[s], 16 * (i + 2))
                    else:
                        pe.wait_ge(e_loaded[s], 16 * (i + 1))
                if isinstance(i, int) and i == FIRST and u < 2:
                    pe.wait_ge(hT_ready, NPAIR + 1)
                else:
                    pe.wait_ge(eT_ready, k - 1)
                for t in range(4):
                    j = 4 * (u % 2) + t
                    last = nc.tensor.transpose(ps_T[u % 2][:, t, :], e_sb[:, s, j * K:(j + 1) * K], ident[:])
                last.then_inc(e_turned, 1)

            def edge_product(i, u, r):
                m = 8 * i + 2 * u + r
                if r == 0:
                    pe.wait_ge(eT_ready, 4 * i + u + 1)
                if isinstance(i, int) and i == FIRST and u == 0:
                    pe.wait_ge(node_copied, NPAIR + 1)
                else:
                    pe.wait_ge(edge_added, m - 1)
                for t in range(2):
                    last = nc.tensor.matmul(ps_E[r][:, t, :], eT_sb[:, u % 2, 2 * r + t, :], we_sb[:],
                                            start=True, stop=True)
                last.then_inc(edge_mm, 1)

            def sum_pair(i, u, r):
                k, m = 4 * i + u, 8 * i + 2 * u + r
                if r == 0:
                    pe.wait_ge(sel_ready, k + 1)
                    if not (isinstance(i, int) and i == FIRST and u < 2):
                        pe.wait_ge(flushed, k)
                pe.wait_ge(msg_ready, m + 1)
                for t in range(2):
                    for h in range(H):
                        last = nc.tensor.matmul(ps_A[u % 2][:, h, 0:WIN],
                                                msg[:, 2 * (u % 2) + r, t, h * P:(h + 1) * P],
                                                sel[:, u % 2, 2 * r + t, :],
                                                start=(r == 0 and t == 0 and h == 0),
                                                stop=(r == 1 and t == 1), skip_group_check=True)
                last.then_inc(seg_done, 1)

            def edge_iteration(i):
                last = isinstance(i, int) and i == IT - 1
                for u in range(3 if last else 4):
                    edge_product(i, u, 0)
                    if not (isinstance(i, int) and i == FIRST and u == 0):
                        sum_pair(*((i, u - 1) if u else (i - 1, 3)), 1)
                    if not (last and u == 2):
                        turn_edges(*((i, u + 1) if u < 3 else (i + 1, 0)))
                    edge_product(i, u, 1)
                    sum_pair(i, u, 0)
            def edge_iterations(lo, hi):
                with pe.Fori(lo, hi) as i:
                    edge_iteration(i)

            def out_product(sums, turned, tiles=2):
                for t in range(tiles):
                    for h in range(H):
                        last = nc.tensor.matmul(sums[:, t * D:(t + 1) * D], turned(h, t), wo_sb[:, h, :],
                                                start=(h == 0), stop=(h == H - 1))
                return last
            pe.wait_ge(weights_loaded, 32)
            turn_edges(0, 0)
            edge_iteration(0)
            nc.tensor.sem_inc(out_mm, 1)
            edge_iterations(1, 8)
            with pe.Fori(2, NBLK) as b:
                edge_iterations(b * 4, b * 4 + 2)
                pe.wait_ge(aT_ready, b - 1)
                pe.wait_ge(out_ready, b - 1)
                out_product(ps_B[0], lambda h, t: aT_sb[:, h, t, :]).then_inc(out_mm, 1)
                edge_iterations(b * 4 + 2, b * 4 + 4)
            edge_iteration(IT - 1)
            sum_pair(IT - 1, 2, 1)
            pe.wait_ge(farmax_ready, 1)
            nc.tensor.transpose(ps_B[1][0:1, 0:P], farmax[:], ident[:]).then_inc(farT_ready, 1)

            pe.wait_ge(flag_ready, 1)
            flag = pe.value_load(far_flag[0:1, 0:1], min_val=0, max_val=N)
            with pe.If(flag > 0):
                with pe.Fori(0, -(-E // P)) as tau:
                    pe.wait_ge(g_loaded, 64 * (tau + 1))
                    nc.tensor.transpose(ps_T[0][:, 0, :], e_sb[:, 0, 0:K], ident[:]).then_inc(g_eT, 1)
                    pe.wait_ge(g_eTc, tau + 1)
                    nc.tensor.matmul(ps_E[0][:, 0, :], eT_sb[:, 0, 0, :], we_sb[:], start=True, stop=True
                                     ).then_inc(g_mm, 1)
                    with pe.Fori(0, NB) as b:
                        pe.wait_ge(g_sel, 2 * (tau * NB + b) + 1)
                        for h in range(H):
                            last = nc.tensor.matmul(ps_B[h][:], msg[:, 0, 0, h * P:(h + 1) * P],
                                                    far_sel[:], start=True, stop=True)
                        last.then_inc(g_sum, 1)

            pe.wait_ge(last_go, 1)
            redo = pe.value_load(redo_flag[0:1, 0:1], min_val=0, max_val=N)
            with pe.If(redo > 0):
                with pe.Fori(0, EARLY) as v:
                    pe.wait_ge(redo_aT, v + 1)
                    out_product(ps_B[0], lambda h, t: aT_sb[:, h, t, :]).then_inc(redo_mm, 1)
            pe.wait_ge(last_aT, 1)
            out_product(ps_B[0], lambda h, t: aT_sb[:, h, t, :]).then_inc(last_mm, 1)
            pe.wait_ge(last_aT, 2)
            out_product(ps_E[0].rearrange("p t d -> p (t d)"), lambda h, t: eT_sb[:, 0, h, :], tiles=1).then_inc(last_mm, 1)


_INS = ["x", "src", "dst", "edge_attr_128", "L0_gnn_W_node", "L0_gnn_b_node", "L0_gnn_W_edge", "L0_gnn_b_edge",
        "L0_gnn_W_out", "L0_gnn_b_out"]


def kernel(x, src, dst, edge_attr_128, L0_gnn_W_node, L0_gnn_b_node, L0_gnn_W_edge, L0_gnn_b_edge, L0_gnn_W_out,
           L0_gnn_b_out):
    import concourse.bacc as bacc
    from concourse import mybir
    from concourse.bass_utils import run_bass_kernel_spmd as run

    nc = bacc.Bacc("TRN2", target_bir_lowering=False, num_devices=1)
    values = (x, src, dst, edge_attr_128, L0_gnn_W_node, L0_gnn_b_node, L0_gnn_W_edge, L0_gnn_b_edge, L0_gnn_W_out,
              L0_gnn_b_out)
    arrays = {f"in_{n}": np.ascontiguousarray(a) for n, a in zip(_INS, values)}
    args = [nc.dram_tensor(n, a.shape, mybir.dt.from_np(a.dtype), kind="ExternalInput").ap() for n, a in arrays.items()]
    out = nc.dram_tensor("out", tuple(x.shape), mybir.dt.float32, kind="ExternalOutput").ap()
    gnn_program(nc, *args, out)
    return run(nc, [arrays], core_ids=[0]).results[0]["out"]
```

```python
import numpy as np


def gnn_program(nc, x, src, dst, edge_attr, w_node, b_node, w_edge, b_edge, w_out, b_out, out):
    import concourse.bass as bass
    from concourse import mybir
    from contextlib import ExitStack

    F32, I32 = mybir.dt.float32, mybir.dt.int32
    ALU = mybir.AluOpType
    ACT = mybir.ActivationFunctionType
    AX = mybir.AxisListType

    P = 128
    N, D = x.shape
    E, K = edge_attr.shape
    H = D // P
    EPS = 1e-5
    TPG = 8
    GE = TPG * P
    G = -(-E // GE)
    GF = E // GE
    GTAIL = E - GF * GE
    QE = 4 * P
    KQ = -(-E // QE)
    WIN = 80
    IE = 2 * GE
    NT = -(-N // P)
    NTAIL = N - (NT - 1) * P
    NQ = -(-NT // 4)
    NPAIR = NT // 2
    BW = 512
    NB = -(-N // BW)
    AW = max(NB * BW, 2 * IE)
    TT = 4
    IT = G // 2
    NBLK = IT // 4
    PER = 2 * P
    EARLY = NBLK - 2
    assert G % 2 == 0 and NT % 8 == 1 and AW >= N + WIN and 0 < GTAIL <= QE
    assert D == 2 * P
    assert IT == 4 * NBLK + 1 and NBLK >= 3 and EARLY == NPAIR - 1

    ctx = ExitStack()
    with ctx:
        def sb(name, shape, dt=F32):
            return ctx.enter_context(nc.sbuf_tensor(name, shape, dt))

        def ps(name, shape, dt=F32):
            return ctx.enter_context(nc.psum_tensor(name, shape, dt))

        def sem(name):
            return ctx.enter_context(nc.semaphore(name))

        node_table = nc.dram_tensor("node_table", (N, D), F32, kind="Internal").ap()

        x_sb = sb("x_sb", [P, NQ * 4 * D])
        aggT = sb("aggT", [P, H, AW])
        gathered = sb("gathered", [P, 2, TPG, D])
        h_sb = gathered[:, :, 0:4, :]
        e_sb = sb("e_sb", [P, 2, TPG * K])
        eT_sb = sb("eT_sb", [P, 2, 4, P])
        msg = sb("msg", [P, 4, 2, D])
        sel = sb("sel", [P, 2, 4, WIN])
        far_sel = sb("far_sel", [P, BW])
        idx_rows = aggT[:, 0, 0:2 * IE].rearrange("p (a e) -> p a e", a=2).bitcast(I32)
        idx_nums = aggT[:, 1, 0:2 * IE].rearrange("p (a e) -> p a e", a=2)
        src_all = sb("src_all", [P, 16, IT], I32)
        src_stage = sb("src_stage", [P, 2, TPG], I32)
        dst_f = sb("dst_f", [P, 16, IT])
        rel = sb("rel", [P, 16, IT])
        far = sb("far", [P, 16, IT])
        base_f = sb("base_f", [P, 4, IT])
        base_i = sb("base_i", [1, IT, 4], I32)
        wn_sb = sb("wn_sb", [P, H, D])
        we_sb = sb("we_sb", [P, D])
        wo_sb = sb("wo_sb", [P, H, D])
        ident = sb("ident", [P, P])
        iota_w = sb("iota_w", [P, BW])
        ones = sb("ones", [1, P])
        bias2 = sb("bias2", [P, 3, 2, D])
        aT_sb = sb("aT_sb", [P, H, 2, P])
        out_sb = sb("out_sb", [P, 2, D])
        settle_at = sb("settle_at", [1, 16 * (NBLK + 1)], I32)
        early = sb("early", [1, 3, 4 * IT])
        early_max = sb("early_max", [1, 2])
        eps_col = sb("eps_col", [P, 1])
        eps_root = sb("eps_root", [P, 1])
        stat = sb("stat", [P, 2, 4, 6])
        mv = sb("mv", [P, 2, 4, 2])
        std = sb("std", [P, 2, 4])
        rstd = sb("rstd", [P, 2, 4])
        nmr = sb("nmr", [P, 2, 4])
        farmax = sb("farmax", [P, 1])
        farmax1 = sb("farmax1", [1, 1])
        far_flag = sb("far_flag", [1, 1], I32)
        redo_flag = sb("redo_flag", [1, 1], I32)
        s_idx = sb("s_idx", [P, 3], I32)
        s_f = sb("s_f", [P, 8])

        ps_T = [ps(f"ps_T{i}", [P, 4, P]) for i in range(2)]
        ps_E = [ps(f"ps_E{i}", [P, 2, D]) for i in range(2)]
        ps_A = [ps(f"ps_A{i}", [P, H, 256]) for i in range(2)]
        ps_B = [ps(f"ps_B{i}", [P, BW]) for i in range(2)]

        consts_set = sem("consts_set")
        ident_zero = sem("ident_zero")
        wn_loaded = sem("wn_loaded")
        weights_loaded = sem("weights_loaded")
        bias_loaded = sem("bias_loaded")
        idx_set = sem("idx_set")
        src_ready = sem("src_ready")
        dst_ready = sem("dst_ready")
        base_copied = sem("base_copied")
        rel_ready = sem("rel_ready")
        far_ready = sem("far_ready")
        eps_set = sem("eps_set")
        x_padded = sem("x_padded")
        prep = sem("prep")
        base_ready = sem("base_ready")
        farT_ready = sem("farT_ready")
        farmax_ready = sem("farmax_ready")
        flag_ready = sem("flag_ready")
        x_loaded = [sem(f"x_loaded{z}") for z in range(2)]
        stats_done = sem("stats_done")
        moments_done = sem("moments_done")
        std_done = sem("std_done")
        rstd_done = sem("rstd_done")
        scale_ready = sem("scale_ready")
        h_ready = sem("h_ready")
        h_turned = sem("h_turned")
        hT_ready = sem("hT_ready")
        node_mm = sem("node_mm")
        node_copied = sem("node_copied")
        node_stored = [sem(f"node_stored{z}") for z in range(2)]
        e_loaded = [sem(f"e_loaded{z}") for z in range(2)]
        idx_staged = sem("idx_staged")
        gather_turn = sem("gather_turn")
        vector_turn = sem("vector_turn")
        rows_landed = [[sem(f"rows_landed{s}{h}") for h in range(2)] for s in range(2)]
        e_turned = sem("e_turned")
        eT_ready = sem("eT_ready")
        edge_mm = sem("edge_mm")
        idx_loaded = sem("idx_loaded")
        src_cast = sem("src_cast")
        dst_cast = sem("dst_cast")
        idx_turned = sem("idx_turned")
        edge_added = sem("edge_added")
        msg_ready = sem("msg_ready")
        sel_ready = sem("sel_ready")
        seg_done = sem("seg_done")
        flushed = sem("flushed")
        g_go = sem("g_go")
        g_loaded = sem("g_loaded")
        g_turn = sem("g_turn")
        g_rows = sem("g_rows")
        g_eT = sem("g_eT")
        g_eTc = sem("g_eTc")
        g_mm = sem("g_mm")
        g_chain = sem("g_chain")
        g_sel = sem("g_sel")
        g_sum = sem("g_sum")
        g_add = sem("g_add")
        aT_ready = sem("aT_ready")
        out_mm = sem("out_mm")
        x_biased = sem("x_biased")
        out_ready = sem("out_ready")
        out_stored = sem("out_stored")
        redo_go = sem("redo_go")
        redo_aT = sem("redo_aT")
        redo_mm = sem("redo_mm")
        redo_ready = sem("redo_ready")
        redo_stored = sem("redo_stored")
        last_go = sem("last_go")
        last_aT = sem("last_aT")
        last_tile_aT = sem("last_tile_aT")
        last_mm = sem("last_mm")
        last_ready = sem("last_ready")
        last_stored = sem("last_stored")

        FIRST = 0
        LAST = NPAIR // 4 - 1

        def xt(t, n=1):
            return x_sb[:, bass.ds(t * D, n * D)]

        def rows_of(ap, first, tiles):
            return ap[bass.ds(first * P, tiles * P), :].rearrange("(t p) d -> p t d", p=P)

        block = ctx.enter_context(nc.Block())

        @block.sync
        def _(sp):
            sp.dma_start(wn_sb[:], w_node.rearrange("(h p) d -> p h d", p=P)).then_inc(wn_loaded, 16)
            sp.wait_ge(idx_set, 2)
            for a, arr in enumerate((src, dst)):
                sp.dma_start(idx_rows[0:IT - 1, a, :], arr[0:(IT - 1) * IE].rearrange("(r e) -> r e", e=IE)
                             ).then_inc(idx_loaded, 16)
                sp.dma_start(idx_rows[IT - 1:IT, a, 0:E - (IT - 1) * IE],
                             arr[(IT - 1) * IE:E].rearrange("(r e) -> r e", r=1)).then_inc(idx_loaded, 16)
            for k, b in enumerate((b_node, b_edge, b_out)):
                for t in range(2):
                    sp.dma_start(bias2[:, k, t, :], b.rearrange("(a d) -> a d", a=1).to_broadcast([P, D])
                                 ).then_inc(bias_loaded, 16)
            sp.dma_start(we_sb[:], w_edge).then_inc(weights_loaded, 16)
            sp.dma_start(wo_sb[:], w_out.rearrange("(h p) d -> p h d", p=P)).then_inc(weights_loaded, 16)
            for s in range(2):
                sp.dma_start(e_sb[:, s, :].rearrange("p (c n) -> p c n", c=2),
                             edge_attr[s * GE:(s + 1) * GE, :].rearrange("(c p j) k -> p c (j k)", c=2, j=4)
                             ).then_inc(e_loaded[s], 16)

            def store_pair(i, u):
                v = 4 * i + u
                sp.wait_ge(node_copied, v + 1)
                sp.dma_start(rows_of(node_table, 2 * v, 2), msg[:, u % 2, :, :]).then_inc(node_stored[u % 2], 16)
            for u in range(4):
                store_pair(0, u)
            with sp.Fori(1, NPAIR // 4) as i:
                for u in range(4):
                    store_pair(i, u)
            sp.wait_ge(node_copied, NPAIR + 1)
            sp.dma_start(node_table[N - NTAIL:N, :], msg[0:NTAIL, 0, 0, :]).then_inc(node_stored[0], 16)

            def load_edges(i, s):
                g = 2 * i + s
                sp.wait_ge(e_turned, 2 * g - 2)
                sp.dma_start(e_sb[:, s, :].rearrange("p (c n) -> p c n", c=2),
                             edge_attr[bass.ds(g * GE, GE), :].rearrange("(c p j) k -> p c (j k)", c=2, j=4)
                             ).then_inc(e_loaded[s], 16)
            with sp.Fori(1, G // 2 - 1) as i:
                load_edges(i, 0)
                load_edges(i, 1)
            load_edges(G // 2 - 1, 0)
            tp, tr = GTAIL // TT, GTAIL % TT
            sp.wait_ge(e_turned, 2 * (G - 1) - 2)
            sp.dma_start(e_sb[0:tp, 1, 0:TT * K], edge_attr[GF * GE:GF * GE + tp * TT, :].rearrange("(p j) k -> p (j k)", j=TT)
                         ).then_inc(e_loaded[1], 16)
            sp.dma_start(e_sb[tp:tp + 1, 1, 0:tr * K], edge_attr[E - tr:E, :].rearrange("(p j) k -> p (j k)", p=1)
                         ).then_inc(e_loaded[1], 16)

            sp.wait_ge(flag_ready, 1)
            flag = sp.value_load(far_flag[0:1, 0:1], min_val=0, max_val=N)
            with sp.If(flag > 0):
                def load_tile(k, j, n):
                    tau = k * 4 + j
                    e0 = k * QE + j * P
                    sp.wait_ge(g_go, tau + 1)
                    sp.dma_start(e_sb[0:n, 0, 0:K], edge_attr[bass.ds(e0, n), :]).then_inc(g_loaded, 16)
                    sp.dma_start(s_idx[0:n, 0:1], src[bass.ds(e0, n)].rearrange("(p a) -> p a", a=1)).then_inc(g_loaded, 16)
                    sp.dma_start(s_idx[0:n, 1:2], dst[bass.ds(e0, n)].rearrange("(p a) -> p a", a=1)).then_inc(g_loaded, 16)
                    sp.dma_start(s_idx[:, 2:3], dst[bass.ds(k * QE, 1)].rearrange("(p a) -> p a", a=1)
                                 .to_broadcast([P, 1])).then_inc(g_loaded, 16)
                with sp.Fori(0, E // QE) as k:
                    with sp.Fori(0, 4) as j:
                        load_tile(k, j, P)
                for j in range(-(-(E % QE) // P)):
                    load_tile(E // QE, j, min(P, E % QE - j * P))

            sp.wait_ge(last_ready, 1)
            sp.dma_start(rows_of(out, 2 * EARLY, 2), out_sb[:]).then_inc(last_stored, 16)
            sp.wait_ge(last_ready, 2)
            sp.dma_start(out[N - NTAIL:N, :], msg[0:NTAIL, 0, 0, :]).then_inc(last_stored, 16)
            sp.wait_ge(last_stored, 32)

        @block.gpsimd
        def _(pool):
            def load_x(i, z):
                w = 2 * i + z
                pool.dma_start(xt(4 * w, 4).rearrange("p (t d) -> p t d", d=D), rows_of(x, 4 * w, 4)
                               ).then_inc(x_loaded[z], 16)
            load_x(0, 0)
            load_x(0, 1)
            pool.memset(idx_rows[:, 0, E - (IT - 1) * IE:IE], 0).then_inc(idx_set, 1)
            pool.memset(idx_rows[:, 1, E - (IT - 1) * IE:IE], -1).then_inc(idx_set, 1)
            pool.memset(ident[:], 0.0).then_inc(ident_zero, 1)
            pool.wait_ge(ident_zero, 1)
            pool.affine_select(out=ident[:], in_=ident[:], compare_op=ALU.not_equal, fill=1.0, base=0,
                               pattern=[[-1, P]], channel_multiplier=1).then_inc(consts_set, 1)
            pool.memset(x_sb[:, (NT - 1) * D:], 0.0).then_inc(x_padded, 1)
            pool.memset(ones[:], 1.0).then_inc(consts_set, 1)
            pool.iota(iota_w[:], pattern=[[1, BW]], base=0, channel_multiplier=0,
                      allow_small_or_imprecise_dtypes=True).then_inc(consts_set, 1)
            pool.iota(settle_at[:], pattern=[[PER, NBLK + 1], [0, 16]], base=-PER, channel_multiplier=0
                      ).then_inc(consts_set, 1)

            with pool.Fori(1, NQ // 2) as i:
                for z in range(2):
                    pool.wait_ge(x_loaded[z], 16 * i)
                    pool.sem_inc(gather_turn, 1)
                    load_x(i, z)
            pool.wait_ge(x_padded, 1)
            pool.wait_ge(x_loaded[0], 16 * (NQ // 2))
            pool.dma_start(x_sb[0:NTAIL, (NT - 1) * D:NT * D], x[N - NTAIL:N, :]).then_inc(x_loaded[0], 16)
            pool.wait_ge(idx_turned, 8)
            pool.memset(aggT[:], 0.0).then_inc(consts_set, 1)

            pool.wait_ge(dst_ready, 4)
            pool.wait_ge(base_copied, 1)
            for c in range(4):
                pool.tensor_tensor(rel[:, 4 * c:4 * c + 4, :], dst_f[:, 4 * c:4 * c + 4, :],
                                   base_f[:, c, :].unsqueeze(1).to_broadcast([P, 4, IT]), ALU.subtract
                                   ).then_inc(rel_ready, 1)
            pool.tensor_copy(base_i[:], base_f[0:1, :, :].rearrange("a c r -> a r c")).then_inc(rel_ready, 1)
            pool.wait_ge(rel_ready, 5)
            pool.tensor_scalar(far[:], rel[:], 0.0, float(WIN - 1), ALU.max, ALU.min).then_inc(far_ready, 1)
            pool.wait_ge(far_ready, 1)
            pool.tensor_tensor(far[:], far[:], rel[:], ALU.subtract).then_inc(far_ready, 1)
            pool.wait_ge(far_ready, 2)
            pool.tensor_tensor(far[:], far[:], far[:], ALU.mult).then_inc(far_ready, 1)

            pool.wait_ge(node_stored[0], 16 * (NPAIR // 2 + 1))
            pool.wait_ge(node_stored[1], 16 * (NPAIR // 2))

            def gather(i, s, tiles=TPG):
                pool.wait_ge(idx_staged, 2 * i + s + 1)
                for j in range(tiles):
                    if j % 4 == 0:
                        if not (isinstance(i, int) and i == FIRST):
                            pool.wait_ge(msg_ready, 8 * i + 4 * s + 2 * (j // 4) - 6)
                        pool.sem_inc(gather_turn, 1)
                    pool.indirect_dma_start(out=gathered[:, s, j, :], out_offset=None, in_=node_table,
                                            in_offset=bass.IndirectOffsetOnAxis(ap=src_stage[:, s, j:j + 1], axis=0)
                                            ).then_inc(rows_landed[s][j // 4], 16)
            gather(0, 0)
            gather(0, 1)
            with pool.Fori(1, IT - 1) as i:
                gather(i, 0)
                gather(i, 1)
            gather(IT - 1, 0)
            gather(IT - 1, 1, TT)

            pool.wait_ge(flag_ready, 1)
            flag = pool.value_load(far_flag[0:1, 0:1], min_val=0, max_val=N)
            with pool.If(flag > 0):
                def gather_tile(tau):
                    pool.wait_ge(g_loaded, 64 * (tau + 1))
                    pool.sem_inc(g_turn, 1)
                    pool.indirect_dma_start(out=gathered[:, 0, 0, :], out_offset=None, in_=node_table,
                                            in_offset=bass.IndirectOffsetOnAxis(ap=s_idx[:, 0:1], axis=0)
                                            ).then_inc(g_rows, 16)
                with pool.Fori(0, -(-E // P)) as tau:
                    gather_tile(tau)

        @block.scalar
        def _(act):
            def deviation(i, z):
                act.wait_ge(moments_done, 2 * i + z + 1)
                nc.scalar.activation(std[:, z, :], mv[:, z, :, 1], ACT.Sqrt, bias=eps_col[:, 0:1]).then_inc(std_done, 1)

            def normalise(i, u):
                v = 4 * i + u
                z = u // 2
                act.wait_ge(scale_ready, 2 * i + z + 1)
                if not (isinstance(i, int) and i == FIRST):
                    act.wait_ge(h_turned, v - 3)
                for t in range(2):
                    last = nc.scalar.activation(h_sb[:, z, 2 * (u % 2) + t, :], xt(2 * v + t), ACT.Relu,
                                                bias=nmr[:, z, 2 * (u % 2) + t:2 * (u % 2) + t + 1],
                                                scale=rstd[:, z, 2 * (u % 2) + t:2 * (u % 2) + t + 1])
                last.then_inc(h_ready, 1)

            def copy_hT(i, u):
                v = 4 * i + u
                act.wait_ge(h_turned, v + 1)
                if not (isinstance(i, int) and i == FIRST and u < 2):
                    act.wait_ge(node_mm, v - 1)
                nc.scalar.copy(eT_sb[:, u % 2, :, :], ps_T[u % 2][:]).then_inc(hT_ready, 1)

            def node_iteration(i):
                last = isinstance(i, int) and i == LAST
                for u in range(4):
                    copy_hT(*((i, u + 1) if u < 3 else (i + 1, 0)))
                    if not (last and u > 1):
                        normalise(*((i, 3) if u == 0 else (i + 1, u - 1)))
                    if u % 2 == 0 and not (last and u == 2):
                        deviation(i + 1, u // 2)

            def node_iterations(lo, hi):
                if lo < min(hi, LAST):
                    with act.Fori(lo, min(hi, LAST)) as i:
                        node_iteration(i)

            def take_table(table, ready):
                for c in range(2):
                    nc.scalar.copy(table[:, 4 * c:4 * c + 4, :], ps_A[c][:].rearrange("p a b -> p (a b)")[:, 0:4 * IT]
                                   .rearrange("p (t r) -> p t r", t=4)).then_inc(ready, 1)
            act.wait_ge(eps_set, 1)
            nc.scalar.activation(eps_root[:], eps_col[:], ACT.Sqrt)
            deviation(0, 0)
            normalise(0, 0)
            normalise(0, 1)
            deviation(0, 1)
            normalise(0, 2)
            copy_hT(0, 0)
            act.wait_ge(idx_loaded, 64)
            nc.scalar.copy(idx_nums[0:IT, 0, :], idx_rows[0:IT, 0, :]).then_inc(src_cast, 1)
            node_iteration(0)
            act.wait_ge(idx_turned, 4)
            take_table(src_all, src_ready)
            node_iterations(1, 2)
            act.wait_ge(idx_turned, 8)
            take_table(dst_f, dst_ready)
            node_iterations(2, 3)
            act.wait_ge(base_ready, 1)
            nc.scalar.copy(base_f[:], ps_B[0][:, 0:4 * IT].rearrange("p (c r) -> p c r", c=4)).then_inc(base_copied, 1)
            node_iterations(3, LAST)
            node_iteration(LAST)

            def copy_eT(i, u):
                k = 4 * i + u
                act.wait_ge(e_turned, k + 1)
                if isinstance(i, int) and i == FIRST and u < 2:
                    act.wait_ge(node_mm, NPAIR + 1)
                else:
                    act.wait_ge(edge_mm, 2 * k - 2)
                nc.scalar.copy(eT_sb[:, u % 2, :, :], ps_T[u % 2][:]).then_inc(eT_ready, 1)
            def copies(lo, hi):
                with act.Fori(lo, hi) as i:
                    for u in range(4):
                        copy_eT(i, u)
            for u in range(4):
                copy_eT(0, u)
            copies(1, 8)
            with act.Fori(2, NBLK) as b:
                copies(b * 4, b * 4 + 1)
                act.wait_ge(flushed, 16 * b + 4)
                act.wait_ge(out_mm, b - 1)
                nc.scalar.copy(aT_sb[:].rearrange("p h t n -> p h (t n)"),
                               aggT[:, :, bass.ds(b * PER - 2 * PER, PER)]).then_inc(aT_ready, 1)
                copies(b * 4 + 1, b * 4 + 4)
                act.wait_ge(out_ready, b)
                act.dma_start(rows_of(out, 2 * b - 4, 2), out_sb[:]).then_inc(out_stored, 16)
            act.wait_ge(flag_ready, 1)
            flag = act.value_load(far_flag[0:1, 0:1], min_val=0, max_val=N)
            redo = act.value_load(redo_flag[0:1, 0:1], min_val=0, max_val=N)
            for u in range(3):
                copy_eT(IT - 1, u)

            with act.If(flag > 0):
                with act.Fori(0, -(-E // P)) as tau:
                    act.wait_ge(g_eT, tau + 1)
                    nc.scalar.copy(eT_sb[:, 0, 0, :], ps_T[0][:, 0, :]).then_inc(g_eTc, 1)

            with act.If(redo > 0):
                with act.Fori(0, EARLY) as v:
                    act.wait_ge(redo_go, v + 1)
                    nc.scalar.copy(aT_sb[:].rearrange("p h t n -> p h (t n)"),
                                   aggT[:, :, bass.ds(v * PER, PER)]).then_inc(redo_aT, 1)
                    act.wait_ge(redo_ready, v + 1)
                    act.dma_start(rows_of(out, 2 * v, 2), out_sb[:]).then_inc(redo_stored, 16)
            act.wait_ge(last_go, 1)
            nc.scalar.copy(aT_sb[:].rearrange("p h t n -> p h (t n)"),
                           aggT[:, :, EARLY * PER:(EARLY + 1) * PER]).then_inc(last_aT, 1)

        @block.vector
        def _(dve):
            def moments(i, z):
                w = 2 * i + z
                dve.wait_ge(x_loaded[z], 16 * (i + 1))
                if not (isinstance(i, int) and i == FIRST):
                    dve.wait_ge(std_done, w - 1)
                for t in range(4):
                    last = nc.vector.bn_stats(stat[:, z, t, :], xt(4 * w + t))
                last.then_inc(stats_done, 1)
                dve.wait_ge(stats_done, w + 1)
                dve.sem_inc(vector_turn, 1)
                for t in range(4):
                    last = nc.vector.bn_aggr(mv[:, z, t, :], stat[:, z, t, :])
                last.then_inc(moments_done, 1)

            def scales(i, z):
                w = 2 * i + z
                dve.wait_ge(std_done, w + 1)
                if not (isinstance(i, int) and i == FIRST):
                    dve.wait_ge(h_ready, 2 * w - 2)
                nc.vector.reciprocal(rstd[:, z, :], std[:, z, :]).then_inc(rstd_done, 1)
                dve.wait_ge(rstd_done, w + 1)
                nc.vector.scalar_tensor_tensor(out=nmr[:, z, :], in0=mv[:, z, :, 0], scalar=-1.0, in1=rstd[:, z, :],
                                               op0=ALU.mult, op1=ALU.mult).then_inc(scale_ready, 1)

            def copy_nodes(i, u):
                v = 4 * i + u
                dve.wait_ge(node_mm, v + 1)
                if not (isinstance(i, int) and i == FIRST and u < 2):
                    dve.wait_ge(node_stored[u % 2], 16 * (2 * i + u // 2))
                nc.vector.tensor_tensor(msg[:, u % 2, :, :], ps_E[u % 2][:], bias2[:, 0, :, :], ALU.add
                                        ).then_inc(node_copied, 1)

            def node_iteration(i):
                last = isinstance(i, int) and i == LAST
                for z in range(2):
                    if not (isinstance(i, int) and i == FIRST and z == 0):
                        copy_nodes(*((i - 1, 3) if z == 0 else (i, 1)))
                    if not (last and z == 1):
                        moments(i + 1, z)
                    copy_nodes(i, 2 * z)
                    if not (last and z == 1):
                        scales(i + 1, z)

            def node_iterations(lo, hi):
                if lo < min(hi, LAST):
                    with dve.Fori(lo, min(hi, LAST)) as i:
                        node_iteration(i)

            def take_table(table, ready):
                for c in range(2):
                    nc.vector.tensor_copy(table[:, 8 + 4 * c:12 + 4 * c, :], ps_B[c][:, 0:4 * IT]
                                          .rearrange("p (t r) -> p t r", t=4)).then_inc(ready, 1)
            nc.vector.memset(eps_col[:], EPS).then_inc(eps_set, 1)
            moments(0, 0)
            scales(0, 0)
            moments(0, 1)
            scales(0, 1)
            dve.wait_ge(idx_loaded, 64)
            nc.vector.tensor_copy(idx_nums[0:IT, 1, :], idx_rows[0:IT, 1, :]).then_inc(dst_cast, 1)
            dve.wait_ge(bias_loaded, 16 * 6)
            dve.wait_ge(x_padded, 1)
            node_iteration(0)
            dve.wait_ge(idx_turned, 4)
            take_table(src_all, src_ready)
            node_iterations(1, 2)
            dve.wait_ge(idx_turned, 8)
            take_table(dst_f, dst_ready)
            dve.wait_ge(src_ready, 4)
            for s in range(2):
                nc.vector.tensor_copy(src_stage[:, s, :], src_all[:, 8 * s:8 * s + 8, 0]).then_inc(idx_staged, 1)
            node_iterations(2, LAST)
            node_iteration(LAST)
            copy_nodes(LAST, 3)
            dve.wait_ge(node_mm, NPAIR + 1)
            dve.wait_ge(node_stored[0], 16 * (NPAIR // 2))
            nc.vector.tensor_tensor(msg[:, 0, 0, :], ps_E[0][:, 0, :], bias2[:, 0, 0, :], ALU.add).then_inc(node_copied, 1)

            dve.wait_ge(h_ready, NPAIR + 1)
            nc.vector.tensor_tensor(xt(2 * EARLY, 2), xt(2 * EARLY, 2), bias2[:, 2, :, :].rearrange("p t d -> p (t d)"),
                                    ALU.add).then_inc(x_biased, 1)
            nc.vector.tensor_tensor(xt(NT - 1), xt(NT - 1), bias2[:, 2, 0, :], ALU.add).then_inc(x_biased, 1)
            dve.wait_ge(far_ready, 3)
            nc.vector.scalar_tensor_tensor(out=far[:], in0=dst_f[:], scalar=1.0, in1=far[:], op0=ALU.add, op1=ALU.mult
                                           ).then_inc(far_ready, 1)
            dve.wait_ge(far_ready, 4)
            nc.vector.tensor_reduce(farmax[:], far[:].rearrange("p g j -> p (g j)"), AX.X, ALU.max).then_inc(farmax_ready, 1)
            dve.wait_ge(rel_ready, 5)
            dve.wait_ge(consts_set, 5)
            nc.vector.tensor_copy(early[0:1, 0, 0:KQ - 2], settle_at[0:1, 0:KQ - 2]).then_inc(prep, 1)
            nc.vector.tensor_copy(early[0:1, 1, :], base_i[0:1, :, :].rearrange("a r c -> a (r c)")).then_inc(prep, 1)
            dve.wait_ge(prep, 2)
            nc.vector.tensor_tensor(early[0:1, 2, 0:KQ - 2], early[0:1, 0, 0:KQ - 2], early[0:1, 1, 2:KQ], ALU.is_gt
                                    ).then_inc(prep, 1)
            dve.wait_ge(prep, 3)
            nc.vector.tensor_reduce(early_max[0:1, 0:1], early[0:1, 2, 0:KQ - 2], AX.X, ALU.max).then_inc(prep, 1)

            def one_hot(i, u):
                k = 4 * i + u
                if not (isinstance(i, int) and i == FIRST and u < 2):
                    dve.wait_ge(seg_done, 2 * k - 2)
                nc.vector.tensor_tensor(sel[:, u % 2, :, :],
                                        iota_w[:, 0:WIN].unsqueeze(1).to_broadcast([P, 4, WIN]),
                                        rel[:, 4 * u:4 * u + 4, bass.ds(i, 1)].to_broadcast([P, 4, WIN]),
                                        ALU.is_equal).then_inc(sel_ready, 1)

            def add_bias(i, u, r):
                m = 8 * i + 2 * u + r
                dve.wait_ge(edge_mm, m + 1)
                if not (isinstance(i, int) and i == FIRST and u < 2):
                    dve.wait_ge(seg_done, m - 3)
                nc.vector.tensor_tensor(msg[:, 2 * (u % 2) + r, :, :], ps_E[r][:], bias2[:, 1, :, :], ALU.add
                                        ).then_inc(edge_added, 1)

            def multiply(i, u, r):
                m = 8 * i + 2 * u + r
                s, h, q = u // 2, u % 2, 2 * (u % 2) + r
                if r == 0:
                    dve.wait_ge(rows_landed[s][h], 64 * (i + 1))
                dve.wait_ge(edge_added, m + 1)
                nc.vector.tensor_tensor(msg[:, q, :, :], msg[:, q, :, :], gathered[:, s, 2 * q:2 * q + 2, :], ALU.mult
                                        ).then_inc(msg_ready, 1)

            def flush(i, u):
                k = 4 * i + u
                base = dve.value_load(base_i[0:1, bass.ds(i, 1), u], min_val=0, max_val=N - 1)
                dve.wait_ge(seg_done, 2 * k + 2)
                dve.wait_ge(flushed, k + 1)
                nc.vector.tensor_tensor(aggT[:, :, bass.ds(base, WIN)], aggT[:, :, bass.ds(base, WIN)],
                                        ps_A[u % 2][:, :, 0:WIN], ALU.add).then_inc(flushed, 1)

            def stage_indices(i, s):
                nc.vector.tensor_copy(src_stage[:, s, :],
                                      src_all[:, 8 * s:8 * s + 8, bass.ds(i + 1, 1)].rearrange("p j a -> p (j a)")
                                      ).then_inc(idx_staged, 1)

            def edge_iteration(i):
                last = isinstance(i, int) and i == IT - 1
                for u in range(3 if last else 4):
                    add_bias(i, u, 0)
                    one_hot(i, u)
                    multiply(i, u, 0)
                    if not (isinstance(i, int) and i == FIRST and u == 0):
                        flush(*((i, u - 1) if u else (i - 1, 3)))
                    add_bias(i, u, 1)
                    if u % 2 == 1 and not last:
                        stage_indices(i, u // 2)
                    multiply(i, u, 1)

            nc.vector.sem_inc(flushed, 1)
            dve.wait_ge(node_stored[0], 16 * (NPAIR // 2 + 1))
            dve.wait_ge(node_stored[1], 16 * (NPAIR // 2))
            edge_iteration(0)

            def edge_iterations(lo, hi):
                with dve.Fori(lo, hi) as i:
                    edge_iteration(i)

            def add_x(v, ready):
                nc.vector.tensor_tensor(out_sb[:].rearrange("p t d -> p (t d)"), ps_B[0][:], xt(2 * v, 2), ALU.add
                                        ).then_inc(ready, 1)

            def block_of_iterations(b):
                nc.vector.tensor_tensor(xt(2 * b - 4, 2), xt(2 * b - 4, 2), bias2[:, 2, :, :].rearrange("p t d -> p (t d)"),
                                        ALU.add).then_inc(x_biased, 1)
                edge_iterations(b * 4, b * 4 + 1)
                dve.wait_ge(aT_ready, b - 1)
                edge_iterations(b * 4 + 1, b * 4 + 3)
                dve.wait_ge(out_mm, b)
                dve.wait_ge(x_biased, b + 1)
                if not isinstance(b, int):
                    dve.wait_ge(out_stored, 16 * (b - 2))
                add_x(b - 2, out_ready)
                edge_iterations(b * 4 + 3, b * 4 + 4)
            nc.vector.sem_inc(out_ready, 1)
            edge_iterations(1, 8)
            dve.wait_ge(farT_ready, 1)
            nc.vector.tensor_reduce(farmax1[:], ps_B[1][0:1, 0:P], AX.X, ALU.max).then_inc(prep, 1)
            dve.wait_ge(prep, 5)
            nc.vector.tensor_scalar(farmax1[:], farmax1[:], 1.0, None, ALU.min).then_inc(prep, 1)
            dve.wait_ge(prep, 6)
            nc.vector.tensor_tensor(early_max[0:1, 1:2], early_max[0:1, 0:1], farmax1[:], ALU.max).then_inc(prep, 1)
            dve.wait_ge(prep, 7)
            nc.vector.tensor_copy(redo_flag[:], early_max[0:1, 1:2]).then_inc(prep, 1)
            dve.wait_ge(prep, 8)
            nc.vector.tensor_copy(far_flag[:], farmax1[:]).then_inc(flag_ready, 1)

            block_of_iterations(2)
            with dve.Fori(3, NBLK) as b:
                block_of_iterations(b)
            dve.wait_ge(flag_ready, 1)
            flag = dve.value_load(far_flag[0:1, 0:1], min_val=0, max_val=N)
            redo = dve.value_load(redo_flag[0:1, 0:1], min_val=0, max_val=N)
            edge_iteration(IT - 1)
            flush(IT - 1, 2)
            dve.wait_ge(flushed, KQ + 1)

            with dve.If(flag > 0):
                CH = 10

                def far_tile(tau):
                    done = [0]

                    def link(ins):
                        done[0] += 1
                        ins.then_inc(g_chain, 1)
                        dve.wait_ge(g_chain, CH * tau + done[0])
                    dve.wait_ge(g_loaded, 64 * (tau + 1))
                    link(nc.vector.tensor_copy(s_f[:, 0:2], s_idx[:, 1:3]))
                    link(nc.vector.tensor_tensor(s_f[:, 2:3], s_f[:, 0:1], s_f[:, 1:2], ALU.subtract))
                    link(nc.vector.tensor_scalar(s_f[:, 3:4], s_f[:, 2:3], 0.0, float(WIN - 1), ALU.max, ALU.min))
                    link(nc.vector.tensor_tensor(s_f[:, 3:4], s_f[:, 3:4], s_f[:, 2:3], ALU.not_equal))
                    link(nc.vector.tensor_scalar(s_f[:, 4:5], s_f[:, 0:1], 1.0, s_f[:, 3:4], ALU.add, ALU.mult))
                    link(nc.vector.tensor_scalar(s_f[:, 5:6], s_f[:, 4:5], -1.0, None, ALU.add))
                    dve.wait_ge(g_mm, tau + 1)
                    dve.wait_ge(g_rows, 16 * (tau + 1))
                    link(nc.vector.tensor_tensor(msg[:, 0, 0, :], ps_E[0][:, 0, :], bias2[:, 1, 0, :], ALU.add))
                    link(nc.vector.tensor_tensor(msg[:, 0, 0, :], msg[:, 0, 0, :], gathered[:, 0, 0, :], ALU.mult))
                    dve.sem_inc(vector_turn, 1)
                    with dve.Fori(0, NB) as b:
                        k = tau * NB + b
                        nc.vector.tensor_scalar(far_sel[:], iota_w[:],
                                                s_f[:, 5:6], None, ALU.is_equal).then_inc(g_sel, 1)
                        dve.wait_ge(g_sel, 2 * k + 1)
                        nc.vector.tensor_scalar(s_f[:, 5:6], s_f[:, 5:6], -float(BW), None, ALU.add).then_inc(g_sel, 1)
                        dve.wait_ge(g_sel, 2 * k + 2)
                        dve.wait_ge(g_sum, k + 1)
                        for h in range(H):
                            last = nc.vector.tensor_tensor(aggT[:, h, bass.ds(b * BW, BW)], aggT[:, h, bass.ds(b * BW, BW)],
                                                           ps_B[h][:], ALU.add)
                        last.then_inc(g_add, 1)
                        dve.wait_ge(g_add, k + 1)
                    link(nc.vector.memset(s_idx[:, 0:1], 0))
                    link(nc.vector.memset(s_idx[:, 1:2], -1))
                    nc.vector.sem_inc(g_go, 1)
                nc.vector.sem_inc(g_go, 1)
                with dve.Fori(0, -(-E // P)) as tau:
                    far_tile(tau)
            dve.wait_ge(out_stored, 16 * EARLY)

            with dve.If(redo > 0):
                nc.vector.sem_inc(redo_go, 1)
                with dve.Fori(0, EARLY) as v:
                    dve.wait_ge(redo_mm, v + 1)
                    add_x(v, redo_ready)
                    dve.wait_ge(redo_stored, 16 * (v + 1))
                    nc.vector.sem_inc(redo_go, 1)
            nc.vector.sem_inc(last_go, 1)
            nc.vector.tensor_copy(eT_sb[:, 0, 0:H, :], aggT[:, :, NPAIR * PER:NPAIR * PER + P]).then_inc(last_tile_aT, 1)
            dve.wait_ge(last_mm, 1)
            add_x(EARLY, last_ready)
            dve.wait_ge(last_mm, 2)
            nc.vector.tensor_tensor(msg[:, 0, 0, :], ps_E[0][:, 0, :], xt(NT - 1), ALU.add).then_inc(last_ready, 1)

        @block.tensor
        def _(pe):
            def turn_h(i, u):
                v = 4 * i + u
                pe.wait_ge(h_ready, v + 1)
                if not (isinstance(i, int) and i == FIRST and u < 2):
                    pe.wait_ge(hT_ready, v - 1)
                for t in range(2):
                    for h in range(H):
                        last = nc.tensor.transpose(ps_T[u % 2][:, 2 * t + h, :],
                                                   h_sb[:, u // 2, 2 * (u % 2) + t, h * P:(h + 1) * P], ident[:])
                last.then_inc(h_turned, 1)

            def node_product(i, u, tiles=2):
                v = 4 * i + u
                pe.wait_ge(hT_ready, v + 1)
                if not (isinstance(i, int) and i == FIRST and u < 2):
                    pe.wait_ge(node_copied, v - 1)
                for t in range(tiles):
                    for h in range(H):
                        last = nc.tensor.matmul(ps_E[u % 2][:, t, :], eT_sb[:, u % 2, 2 * t + h, :], wn_sb[:, h, :],
                                                start=(h == 0), stop=(h == H - 1))
                last.then_inc(node_mm, 1)

            def node_iteration(i):
                for u in range(4):
                    turn_h(*((i, u + 1) if u < 3 else (i + 1, 0)))
                    node_product(i, u)

            def node_iterations(lo, hi):
                if lo < min(hi, LAST):
                    with pe.Fori(lo, min(hi, LAST)) as i:
                        node_iteration(i)

            def turn_indices(a):
                for c, bank in enumerate((ps_A[0], ps_A[1], ps_B[0], ps_B[1])):
                    flat = bank[:] if c > 1 else bank[:].rearrange("p a b -> p (a b)")
                    by_tile = idx_nums[0:IT, a, c * QE:(c + 1) * QE].rearrange("r (p t) -> r t p", t=4)
                    for t in range(4):
                        last = nc.tensor.transpose(flat[:, t * IT:(t + 1) * IT], by_tile[:, t, :], ident[0:IT, 0:IT])
                    last.then_inc(idx_turned, 1)
            pe.wait_ge(consts_set, 4)
            turn_h(0, 0)
            pe.wait_ge(wn_loaded, 16)
            node_iteration(0)
            pe.wait_ge(src_cast, 1)
            turn_indices(0)
            node_iterations(1, 2)
            pe.wait_ge(dst_cast, 1)
            pe.wait_ge(src_ready, 4)
            turn_indices(1)
            node_iterations(2, 3)
            pe.wait_ge(dst_ready, 4)
            nc.tensor.matmul(ps_B[0][:, 0:4 * IT], ones[:], dst_f[0:1, 0:16:4, :], start=True, stop=True
                             ).then_inc(base_ready, 1)
            node_iterations(3, LAST)
            node_iteration(LAST)
            node_product(LAST + 1, 0, tiles=1)

            def turn_edges(i, u):
                k = 4 * i + u
                s = u // 2
                if u % 2 == 0:
                    if isinstance(i, int) and i == IT - 1 and s == 1:
                        pe.wait_ge(e_loaded[s], 16 * (i + 2))
                    else:
                        pe.wait_ge(e_loaded[s], 16 * (i + 1))
                if isinstance(i, int) and i == FIRST and u < 2:
                    pe.wait_ge(hT_ready, NPAIR + 1)
                else:
                    pe.wait_ge(eT_ready, k - 1)
                for t in range(4):
                    j = 4 * (u % 2) + t
                    last = nc.tensor.transpose(ps_T[u % 2][:, t, :], e_sb[:, s, j * K:(j + 1) * K], ident[:])
                last.then_inc(e_turned, 1)

            def edge_product(i, u, r):
                m = 8 * i + 2 * u + r
                if r == 0:
                    pe.wait_ge(eT_ready, 4 * i + u + 1)
                if isinstance(i, int) and i == FIRST and u == 0:
                    pe.wait_ge(node_copied, NPAIR + 1)
                else:
                    pe.wait_ge(edge_added, m - 1)
                for t in range(2):
                    last = nc.tensor.matmul(ps_E[r][:, t, :], eT_sb[:, u % 2, 2 * r + t, :], we_sb[:],
                                            start=True, stop=True)
                last.then_inc(edge_mm, 1)

            def sum_pair(i, u, r):
                k, m = 4 * i + u, 8 * i + 2 * u + r
                if r == 0:
                    pe.wait_ge(sel_ready, k + 1)
                    if not (isinstance(i, int) and i == FIRST and u < 2):
                        pe.wait_ge(flushed, k)
                pe.wait_ge(msg_ready, m + 1)
                for t in range(2):
                    for h in range(H):
                        last = nc.tensor.matmul(ps_A[u % 2][:, h, 0:WIN],
                                                msg[:, 2 * (u % 2) + r, t, h * P:(h + 1) * P],
                                                sel[:, u % 2, 2 * r + t, :],
                                                start=(r == 0 and t == 0 and h == 0),
                                                stop=(r == 1 and t == 1), skip_group_check=True)
                last.then_inc(seg_done, 1)

            def edge_iteration(i):
                last = isinstance(i, int) and i == IT - 1
                for u in range(3 if last else 4):
                    edge_product(i, u, 0)
                    if not (isinstance(i, int) and i == FIRST and u == 0):
                        sum_pair(*((i, u - 1) if u else (i - 1, 3)), 1)
                    if not (last and u == 2):
                        turn_edges(*((i, u + 1) if u < 3 else (i + 1, 0)))
                    edge_product(i, u, 1)
                    sum_pair(i, u, 0)

            def edge_iterations(lo, hi):
                with pe.Fori(lo, hi) as i:
                    edge_iteration(i)

            def out_product(sums, turned, tiles=2):
                for t in range(tiles):
                    for h in range(H):
                        last = nc.tensor.matmul(sums[:, t * D:(t + 1) * D], turned(h, t), wo_sb[:, h, :],
                                                start=(h == 0), stop=(h == H - 1))
                return last
            pe.wait_ge(weights_loaded, 32)
            turn_edges(0, 0)
            edge_iteration(0)
            pe.wait_ge(farmax_ready, 1)
            nc.tensor.transpose(ps_B[1][0:1, 0:P], farmax[:], ident[:]).then_inc(farT_ready, 1)
            nc.tensor.sem_inc(out_mm, 1)
            edge_iterations(1, 8)
            with pe.Fori(2, NBLK) as b:
                edge_iterations(b * 4, b * 4 + 2)
                pe.wait_ge(aT_ready, b - 1)
                pe.wait_ge(out_ready, b - 1)
                out_product(ps_B[0], lambda h, t: aT_sb[:, h, t, :]).then_inc(out_mm, 1)
                edge_iterations(b * 4 + 2, b * 4 + 4)
            pe.wait_ge(flag_ready, 1)
            flag = pe.value_load(far_flag[0:1, 0:1], min_val=0, max_val=N)
            redo = pe.value_load(redo_flag[0:1, 0:1], min_val=0, max_val=N)
            edge_iteration(IT - 1)
            sum_pair(IT - 1, 2, 1)

            with pe.If(flag > 0):
                with pe.Fori(0, -(-E // P)) as tau:
                    pe.wait_ge(g_loaded, 64 * (tau + 1))
                    nc.tensor.transpose(ps_T[0][:, 0, :], e_sb[:, 0, 0:K], ident[:]).then_inc(g_eT, 1)
                    pe.wait_ge(g_eTc, tau + 1)
                    nc.tensor.matmul(ps_E[0][:, 0, :], eT_sb[:, 0, 0, :], we_sb[:], start=True, stop=True
                                     ).then_inc(g_mm, 1)
                    with pe.Fori(0, NB) as b:
                        pe.wait_ge(g_sel, 2 * (tau * NB + b) + 1)
                        for h in range(H):
                            last = nc.tensor.matmul(ps_B[h][:], msg[:, 0, 0, h * P:(h + 1) * P],
                                                    far_sel[:], start=True, stop=True)
                        last.then_inc(g_sum, 1)

            with pe.If(redo > 0):
                with pe.Fori(0, EARLY) as v:
                    pe.wait_ge(redo_aT, v + 1)
                    out_product(ps_B[0], lambda h, t: aT_sb[:, h, t, :]).then_inc(redo_mm, 1)
            pe.wait_ge(last_aT, 1)
            out_product(ps_B[0], lambda h, t: aT_sb[:, h, t, :]).then_inc(last_mm, 1)
            pe.wait_ge(last_tile_aT, 1)
            out_product(ps_E[0].rearrange("p t d -> p (t d)"), lambda h, t: eT_sb[:, 0, h, :], tiles=1).then_inc(last_mm, 1)


_INS = ["x", "src", "dst", "edge_attr_128", "L0_gnn_W_node", "L0_gnn_b_node", "L0_gnn_W_edge", "L0_gnn_b_edge",
        "L0_gnn_W_out", "L0_gnn_b_out"]


def kernel(x, src, dst, edge_attr_128, L0_gnn_W_node, L0_gnn_b_node, L0_gnn_W_edge, L0_gnn_b_edge, L0_gnn_W_out,
           L0_gnn_b_out):
    import concourse.bacc as bacc
    from concourse import mybir
    from concourse.bass_utils import run_bass_kernel_spmd as run

    nc = bacc.Bacc("TRN2", target_bir_lowering=False, num_devices=1)
    values = (x, src, dst, edge_attr_128, L0_gnn_W_node, L0_gnn_b_node, L0_gnn_W_edge, L0_gnn_b_edge, L0_gnn_W_out,
              L0_gnn_b_out)
    arrays = {f"in_{n}": np.ascontiguousarray(a) for n, a in zip(_INS, values)}
    args = [nc.dram_tensor(n, a.shape, mybir.dt.from_np(a.dtype), kind="ExternalInput").ap() for n, a in arrays.items()]
    out = nc.dram_tensor("out", tuple(x.shape), mybir.dt.float32, kind="ExternalOutput").ap()
    gnn_program(nc, *args, out)
    return run(nc, [arrays], core_ids=[0]).results[0]["out"]
```
